# Optimizing a Trainium2 kernel written in Bass

```python
import numpy as np
import jax
import jax.numpy as jnp

def _softmax(x, axis=-1):
    return jax.nn.softmax(x, axis=axis)

def _gelu(x):
    return jax.nn.gelu(x, approximate=True)

def _silu(x):
    return jax.nn.silu(x)

def _sigmoid(x):
    return jax.nn.sigmoid(x)

def _layernorm(x, axis=-1, eps=1e-05):
    m = jnp.mean(x, axis=axis, keepdims=True)
    v = jnp.var(x, axis=axis, keepdims=True)
    return (x - m) / jnp.sqrt(v + eps)

def _scatter_add(tgt, idx, src, axis=0):
    return tgt.at[idx].add(src)

def _segment_sum(src, seg, n):
    return jax.ops.segment_sum(src, seg, n)
kernel_name = 'mk_metaformer_d1_conv_nchw256_r2_1e14a9'

def setup_inputs(seed: int=0):
    np.random.seed(seed)
    _w = jnp.asarray

    def _rec_inputs():
        import jax
        import jax.numpy as jnp
        _gk = jax.random.key(seed)
        x = -0.0002091 + 1 * jax.random.normal(jax.random.fold_in(_gk, 1), (32, 128, 56, 56), jnp.float32)
        return x
    x = _rec_inputs()

    def _L0_conv_setup():
        import jax, jax.numpy as jnp
        import numpy as np
        EPS = 1e-05

        @jax.custom_vjp
        def sign_a(x):
            return jnp.sign(x)

        def _sign_a_fwd(x):
            return (jnp.sign(x), x)

        def _sign_a_bwd(x, g):
            return (g * (jnp.abs(x) <= 1.0).astype(g.dtype),)
        sign_a.defvjp(_sign_a_fwd, _sign_a_bwd)

        @jax.custom_vjp
        def sign_w(x):
            return jnp.sign(x)

        def _sign_w_fwd(x):
            return (jnp.sign(x), None)

        def _sign_w_bwd(_, g):
            return (g,)
        sign_w.defvjp(_sign_w_fwd, _sign_w_bwd)

        def quant_weight_W2(w):
            wc = jnp.clip(w - jnp.mean(w, axis=1, keepdims=True), -1.0, 1.0)
            alpha = jnp.mean(jnp.abs(wc), axis=(1, 2, 3), keepdims=True)
            return sign_w(wc) * alpha
        key = jax.random.key(seed)
        kx, kw, kb, kg, kbt = jax.random.split(key, 5)
        x = jax.random.normal(kx, (32, 128, 56, 56), jnp.float32)
        w = jax.random.normal(kw, (128, 128, 3, 3), jnp.float32) * 0.05
        b = jax.random.normal(kb, (128,), jnp.float32) * 0.01
        gamma = 1.0 + 0.1 * jax.random.normal(kg, (128,), jnp.float32)
        beta = 0.1 * jax.random.normal(kbt, (128,), jnp.float32)
        return {'x': x, 'w': w, 'b': b, 'gamma': gamma, 'beta': beta}
    _L0_conv_all = _L0_conv_setup()
    _L0_conv_in = {k: v for k, v in _L0_conv_all.items() if k in ('w', 'b', 'gamma', 'beta')}
    del _L0_conv_all

    def _L0_ffn_setup():
        import jax, jax.numpy as jnp
        import numpy as np
        B, S, D = (8, 2048, 128)
        H = 4 * D
        CAPACITY = 0.5
        key = jax.random.key(seed)
        ks = jax.random.split(key, 6)
        x = jax.random.normal(ks[0], (B, S, D), dtype=jnp.float32)
        attention_mask = jnp.zeros((B, 1, 1, S), dtype=jnp.float32)
        wr = jax.random.normal(ks[1], (D, 1), dtype=jnp.float32) * 0.02
        br = jnp.zeros((1,), dtype=jnp.float32)
        w1 = jax.random.normal(ks[2], (D, H), dtype=jnp.float32) * 0.02
        b1 = jnp.zeros((H,), dtype=jnp.float32)
        w2 = jax.random.normal(ks[3], (H, D), dtype=jnp.float32) * 0.02
        b2 = jnp.zeros((D,), dtype=jnp.float32)
        return {'x': x, 'attention_mask': attention_mask, 'wr': wr, 'br': br, 'w1': w1, 'b1': b1, 'w2': w2, 'b2': b2}
    _L0_ffn_all = _L0_ffn_setup()
    _L0_ffn_in = {k: v for k, v in _L0_ffn_all.items() if k in ('attention_mask', 'wr', 'br', 'w1', 'b1', 'w2', 'b2')}
    del _L0_ffn_all
    return {'x': x, 'L0_conv_w': _L0_conv_in['w'], 'L0_conv_b': _L0_conv_in['b'], 'L0_conv_gamma': _L0_conv_in['gamma'], 'L0_conv_beta': _L0_conv_in['beta'], 'L0_ffn_attention_mask': _L0_ffn_in['attention_mask'], 'L0_ffn_wr': _L0_ffn_in['wr'], 'L0_ffn_br': _L0_ffn_in['br'], 'L0_ffn_w1': _L0_ffn_in['w1'], 'L0_ffn_b1': _L0_ffn_in['b1'], 'L0_ffn_w2': _L0_ffn_in['w2'], 'L0_ffn_b2': _L0_ffn_in['b2']}

def reference(x, L0_conv_w, L0_conv_b, L0_conv_gamma, L0_conv_beta, L0_ffn_attention_mask, L0_ffn_wr, L0_ffn_br, L0_ffn_w1, L0_ffn_b1, L0_ffn_w2, L0_ffn_b2):
    import jax
    import jax.numpy as jnp

    def _L0_conv_ref(x, w, b, gamma, beta):
        import jax, jax.numpy as jnp
        import numpy as np
        EPS = 1e-05

        @jax.custom_vjp
        def sign_a(x):
            return jnp.sign(x)

        def _sign_a_fwd(x):
            return (jnp.sign(x), x)

        def _sign_a_bwd(x, g):
            return (g * (jnp.abs(x) <= 1.0).astype(g.dtype),)
        sign_a.defvjp(_sign_a_fwd, _sign_a_bwd)

        @jax.custom_vjp
        def sign_w(x):
            return jnp.sign(x)

        def _sign_w_fwd(x):
            return (jnp.sign(x), None)

        def _sign_w_bwd(_, g):
            return (g,)
        sign_w.defvjp(_sign_w_fwd, _sign_w_bwd)

        def quant_weight_W2(w):
            wc = jnp.clip(w - jnp.mean(w, axis=1, keepdims=True), -1.0, 1.0)
            alpha = jnp.mean(jnp.abs(wc), axis=(1, 2, 3), keepdims=True)
            return sign_w(wc) * alpha
        xa = sign_a(x)
        wq = quant_weight_W2(w)
        y = jax.lax.conv_general_dilated(xa, wq, window_strides=(1, 1), padding=[(1, 1), (1, 1)], dimension_numbers=('NCHW', 'OIHW', 'NCHW'))
        y = y + b[None, :, None, None]
        mean = jnp.mean(y, axis=(0, 2, 3), keepdims=True)
        var = jnp.var(y, axis=(0, 2, 3), keepdims=True)
        y = (y - mean) * jax.lax.rsqrt(var + EPS)
        y = y * gamma[None, :, None, None] + beta[None, :, None, None]
        return jax.nn.relu(y)

    def _L0_ffn_ref(x, attention_mask, wr, br, w1, b1, w2, b2):
        import jax, jax.numpy as jnp
        import numpy as np
        B, S, D = (8, 2048, 128)
        H = 4 * D
        CAPACITY = 0.5
        b, s, d = x.shape
        weights = (jnp.einsum('bsd,do->bso', x, wr) + br)[..., 0]
        k = max(1, int(CAPACITY * s))
        kk = k - 1 if k > 1 else 1
        _, idx = jax.lax.top_k(weights, k)
        sel_idx = idx[:, :kk]
        sel = jnp.take_along_axis(x, sel_idx[:, :, None], axis=1)
        h = jax.nn.gelu(jnp.einsum('bkd,dh->bkh', sel, w1) + b1)
        y = jnp.einsum('bkh,hd->bkd', h, w2) + b2
        w_sel = jnp.take_along_axis(weights, sel_idx, axis=1)
        y = y * w_sel[..., None]
        batch_idx = jnp.arange(b)[:, None]
        processed = jnp.zeros_like(x).at[batch_idx, sel_idx].set(y)
        return processed + x

    def _gn(v, G=32, eps=1e-05):
        B_, C_, H_, W_ = v.shape
        g = v.reshape(B_, G, C_ // G, H_, W_)
        m = jnp.mean(g, axis=(2, 3, 4), keepdims=True)
        s = jnp.var(g, axis=(2, 3, 4), keepdims=True)
        return ((g - m) / jnp.sqrt(s + eps)).reshape(v.shape)

    def _ln_c(v, eps=1e-06):
        m = jnp.mean(v, axis=1, keepdims=True)
        s = jnp.var(v, axis=1, keepdims=True)
        return (v - m) / jnp.sqrt(s + eps)

    def _ln_t(v, eps=1e-05):
        m = jnp.mean(v, axis=-1, keepdims=True)
        s = jnp.var(v, axis=-1, keepdims=True)
        return (v - m) / jnp.sqrt(s + eps)

    def _to_tokens(v):
        B_, C_, H_, W_ = v.shape
        return v.reshape(B_, C_, H_ * W_).transpose(0, 2, 1)

    def _from_tokens(t, like):
        B_, C_, H_, W_ = like.shape
        return t.transpose(0, 2, 1).reshape(B_, C_, H_, W_)
    x = x + _L0_conv_ref(_ln_c(x), L0_conv_w, L0_conv_b, L0_conv_gamma, L0_conv_beta)
    t = _to_tokens(x)
    t = t + _L0_ffn_ref(_ln_t(t), L0_ffn_attention_mask, L0_ffn_wr, L0_ffn_br, L0_ffn_w1, L0_ffn_b1, L0_ffn_w2, L0_ffn_b2)
    x = _from_tokens(t, x)
    return x

_drawn_inputs = setup_inputs


def setup_inputs(seed=0):
    import zlib

    import numpy as np

    out = dict(_drawn_inputs(seed))
    spreads = {'L0_ffn_b1': (0.0, 0.8), 'L0_ffn_b2': (0.0, 0.8)}
    factors = {'L0_conv_b': 8.0, 'L0_ffn_wr': 8.0, 'L0_ffn_w1': 8.0, 'L0_ffn_w2': 8.0}
    for name, (base, spread) in spreads.items():
        noise = np.random.default_rng([zlib.crc32(name.encode()), seed]).standard_normal(out[name].shape)
        drawn = base * np.exp(spread * noise) if base else spread * noise
        out[name] = jnp.asarray(drawn.astype(out[name].dtype))
    for name, factor in factors.items():
        out[name] = (out[name] * factor).astype(out[name].dtype)
    return out
```

```python
import numpy as np
import concourse.bass as bass
from concourse import mybir
from contextlib import ExitStack

C = 128
SIDE = 56
TOK = SIDE * SIDE
ROWS = 8
T = ROWS * SIDE
NCH = TOK // T
TAPS = 9
PAD = SIDE + 2
TILE = 112
NT = TOK // TILE
TPG = T // TILE
HID = 512
NB = HID // C
TOP = max(1, int(0.5 * TOK)) - 1
CAND = 16
SUB = C // CAND
SLEN = TOK // SUB
ROUNDS = 8
MR_ROWS, MR_COLS = 98, 32
EPS = 1e-5

K_ID, K_CEN, K_SAME, K_FLAG, K_STRI, K_TRIU, K_ONES, K_CIDX, K_MHALF, K_END = (
    0, 128, 256, 384, 512, 640, 672, 800, 801, 801 + NT)


def constants():
    t = np.zeros((C, K_END), np.float32)
    p, q = np.arange(C)[:, None], np.arange(C)[None, :]
    t[:, K_ID:K_ID + C] = p == q
    t[:, K_CEN:K_CEN + C] = (p == q) - 1.0 / C
    t[:, K_SAME:K_SAME + C] = p % CAND == q % CAND
    t[:, K_FLAG:K_FLAG + C] = (p >= 1) & (p < CAND)
    t[:, K_STRI:K_STRI + C] = p < q
    t[:, K_TRIU:K_TRIU + MR_COLS] = p <= q[:, :MR_COLS]
    t[:, K_ONES:K_ONES + C] = 1.0
    t[:, K_CIDX] = np.arange(C) % CAND
    t[:, K_MHALF:K_END] = -0.5
    return t


POS = 2 * NB * NCH
TRANSPOSE_AT = [0, 2, 4, 8, 10, 12, 14]
WROW_AT = 6
STAT_AT = 17
NORM_AT = [25, 29, 33, 38, 42, 46, 50]
OUT_AT = [5, 9, 13, 17, 21, 27, 31]
COUNT_AT = [16, 20, 24, 28, 32, 36, 41, 45]
INDEX_AT = [18, 22, 26, 30, 34, 39, 43, 47]
MASK_AT = 51
SCAN_AT = 54
RELU_AT = [15, 21, 27, 33, 39, 45, 51]


def block_kernel(nc, consts, x_in, cw_in, cb_in, gamma_in, beta_in, wr_in, br_in, w1_in, b1_in,
                 w2_in, b2_in, out, n_img):
    f32, f32r = mybir.dt.float32, mybir.dt.float32r
    bf16, f16, i32 = mybir.dt.bfloat16, mybir.dt.float16, mybir.dt.int32
    ALU = mybir.AluOpType
    ACT = mybir.ActivationFunctionType
    AX = mybir.AxisListType

    x_v = x_in.rearrange("b c h w -> (b c) (h w)")
    out_v = out.rearrange("b c h w -> (b c) (h w)")
    y_dram = nc.dram_tensor("y_int", [n_img * C, TOK], f16).ap()
    w_dram = nc.dram_tensor("w_row", [n_img, TOK], f32).ap()

    with ExitStack() as ctx:
        def sb(name, shape, dt):
            return ctx.enter_context(nc.sbuf_tensor(name, shape, dt))

        def sem(name):
            return ctx.enter_context(nc.semaphore(name))

        kt = sb("kt", [C, K_END], f32)
        ident = kt[:, K_ID:K_ID + C]
        centre_r = sb("centre_r", [C, C], f32r)
        ones_r = sb("ones_r", [C, C], f32r)
        cwT = sb("cwT", [C, TAPS, C], bf16)
        w1_h = sb("w1_h", [C, HID], f32r)
        w1_l = sb("w1_l", [C, HID], f32r)
        w2_f = sb("w2_f", [C, NB, C], f32)
        b1c = sb("b1c", [C, NB], f32)
        cols = sb("cols", [C, 8], f32)
        cb_c, gamma_c, beta_c, b2_c, wr_c, br_c = (cols[:, i:i + 1] for i in range(6))
        wsel_h = sb("wsel_h", [C, 2 * C], f32r)
        wsel_l = sb("wsel_l", [C, 2 * C], f32r)
        sm = sb("sm", [C, 32], f32)
        (wr2, bound2, bound, half, abs_sum, bn_ve, bn_r, mean_y, bias_d) = (sm[:, i:i + 1] for i in range(9))
        wmean = sm[:, 16:16 + TAPS]
        bn_mv = sm[:, 26:28]
        ident_b = sb("ident_b", [C, C], bf16)
        steps = sb("steps", [C, ROUNDS], f32)
        candc = sb("candc", [C, ROUNDS], f32)
        neg_b = sb("neg_b", [C, 1], f32)
        cand0 = sb("cand0", [C, 1], f32)
        alpha = sb("alpha", [C, 1], f32)
        bn_s = sb("bn_s", [C, 1], f32)
        bn_t = sb("bn_t", [C, 1], f32)

        xb = [sb(f"xb{b}", [C, TOK], f32) for b in range(2)]
        y16 = [sb(f"y16{b}", [C, TOK], f16) for b in range(2)]
        base = [sb(f"base{b}", [C, TOK], f32) for b in range(2)]
        yo = [sb(f"yo{b}", [C, TOK], f32) for b in range(2)]
        th = [sb(f"th{b}", [C, TOK], f32r) for b in range(2)]
        tl = [sb(f"tl{b}", [C, TOK], f32r) for b in range(2)]
        sg = [yo[b][:, 0:PAD * PAD // 2].bitcast(bf16).rearrange("p (r w) -> p r w", w=PAD) for b in range(2)]
        bnst = base[0][:, 0:n_img * NCH * 6].rearrange("p (g s) -> p g s", s=6)

        xh = [sb(f"xh{b}", [C, T], f32r) for b in range(2)]
        xl = [sb(f"xl{b}", [C, T], f32r) for b in range(2)]
        zr = [sb(f"zr{b}", [C, T], f32) for b in range(2)]
        ur = [sb(f"ur{b}", [C, T], f32) for b in range(2)]
        tr = [sb(f"tr{b}", [C, T], f32) for b in range(2)]
        hs = [sb(f"hs{b}", [C, NB, T], f32) for b in range(2)]
        cw, cwc = (h[:, :, :].rearrange("p a b -> p (a b)")[:, 0:C * TAPS] for h in hs)
        cwa = base[1][:, 0:C * TAPS]
        cws = base[1][:, C * TAPS:C * TAPS * 3 // 2].bitcast(bf16).rearrange("o (t i) -> o t i", i=C)
        w1_f = base[1][:, 2 * C * TAPS:2 * C * TAPS + HID]
        rows = sb("rows", [C, TOK], f32r)
        st = sb("st", [TILE, NT, 6], f32)
        stw = sb("stw", [TILE, 6, NT], f32)
        rm = sb("rm", [TILE, 2, NT], f32)
        rms = sb("rms", [NT, 2, 2, TILE], f32r)
        wrow = sb("wrow", [NCH, T], f32)
        wse = sb("wse", [C, SLEN], f32)
        junk = sb("junk", [C, SLEN], bf16)
        wk = sb("wk", [MR_ROWS, MR_COLS], f32)
        mk = sb("mk", [MR_ROWS, 8, MR_COLS], f32)
        mks = sb("mks", [MR_ROWS, 2, MR_COLS], f32r)
        et = sb("et", [MR_COLS, MR_ROWS], f32)
        srch = sb("srch", [C, 16], f32)
        cnt_c, flag_c, lo_c, cand_c, rowg_c, rowe_c, off_c = (srch[:, i:i + 1] for i in range(7))

        ps = ctx.enter_context(nc.psum_tensor("ps", [C, 8, 512], f32))
        H_BANK, Y_BANK, T_BANK, BC0, BC1 = 0, 4, 5, 6, 7
        CEN_BANK, CONV_BANK = 0, 2
        ties_sb = mk[:, 2, :]
        cnt_ps = ps[:, T_BANK, 0:1]
        idx_ps = ps[:, T_BANK, 1:2]
        off_ps = ps[0:MR_ROWS, T_BANK, T:T + 1]

        params_in = sem("params_in")
        prep = sem("prep")
        prep_pool = sem("prep_pool")
        wr2_ready = sem("wr2_ready")
        wr2_summed = sem("wr2_summed")
        bound_ready = sem("bound_ready")
        bound_rooted = sem("bound_rooted")
        cw_centred = sem("cw_centred")
        abs_summed = sem("abs_summed")
        cw_signed = sem("cw_signed")
        cw_transposed = sem("cw_transposed")
        tables_ready = sem("tables_ready")
        var_bn_ready = sem("var_bn_ready")
        bn_rooted = sem("bn_rooted")
        cw_ready = sem("cw_ready")
        border_clear = sem("border_clear")
        x_in_s = [sem(f"x_in{b}") for b in range(2)]
        xh_ready = sem("xh_ready")
        split_ready = sem("split_ready")
        centred = sem("centred")
        signed = sem("signed")
        conv_done = sem("conv_done")
        y_copied = sem("y_copied")
        bn_taken = sem("bn_taken")
        y_saved = [sem(f"y_saved{b}") for b in range(2)]
        coef_ready = sem("coef_ready")
        xy_in = [sem(f"xy_in{b}") for b in range(2)]
        relu_ready = sem("relu_ready")
        x1_ready = sem("x1_ready")
        transposed = sem("transposed")
        stats_taken = sem("stats_taken")
        stat_step = sem("stat_step")
        var_ready = sem("var_ready")
        rstd_ready = sem("rstd_ready")
        mr_ready = sem("mr_ready")
        stat_rows = sem("stat_rows")
        rms_h = sem("rms_h")
        rms_ready = sem("rms_ready")
        norm_rows_in = sem("norm_rows_in")
        bc_stats = sem("bc_stats")
        u_ready = sem("u_ready")
        t_ready = sem("t_ready")
        base_ready = sem("base_ready")
        th_ready = sem("th_ready")
        tl_ready = sem("tl_ready")
        w_done = sem("w_done")
        w_taken = sem("w_taken")
        w_saved = sem("w_saved")
        w_search_in = sem("w_search_in")
        w_mask_in = sem("w_mask_in")
        search_dve = sem("search_dve")
        search_pe = sem("search_pe")
        search_step = sem("search_step")
        mask_step = sem("mask_step")
        ties_ready = sem("ties_ready")
        ties_t = sem("ties_t")
        ties_copied = sem("ties_copied")
        ties_scanned = sem("ties_scanned")
        gate_ready = sem("gate_ready")
        gate_rows_in = sem("gate_rows_in")
        bc_gate = sem("bc_gate")
        h_done = sem("h_done")
        gelu_done = sem("gelu_done")
        y_done = sem("y_done")
        y_taken = sem("y_taken")
        gated = sem("gated")
        out_ready = sem("out_ready")
        out_saved = [sem(f"out_saved{b}") for b in range(2)]

        def wait_count(eng, semaphore, value):
            if not (isinstance(value, int) and value <= 0):
                eng.wait_ge(semaphore, value)

        def pairs(eng, body, first, last, lo, hi):
            for n in range(lo, first):
                body(n, n % 2)
            turns = (last - first) // 2
            with eng.Fori(0, turns) as k:
                body(k * 2 + first, first % 2)
                body(k * 2 + (first + 1), (first + 1) % 2)
            for n in range(first + 2 * turns, hi):
                body(n, n % 2)

        def is_int(n):
            return isinstance(n, int)

        def has(n, low=0, high=n_img):
            return not is_int(n) or low <= n < high

        def cut(t, c, size=T):
            return t[:, c * size:(c + 1) * size]

        P1 = (1, n_img - 1)
        P2 = (1, n_img - 3)

        block = ctx.enter_context(nc.Block())

        @block.sync
        def _(sp):
            sp.dma_start(kt[:, :], consts).then_inc(params_in, 16)
            sp.dma_start(cw, cw_in.rearrange("o i h w -> o (i h w)")).then_inc(params_in, 16)
            for n in range(2):
                sp.dma_start(xb[n][:, :], x_v[n * C:(n + 1) * C, :]).then_inc(x_in_s[n], 16)
            for i, p in enumerate((cb_in, gamma_in, beta_in, b2_in)):
                sp.dma_start(cols[:, i:i + 1], p.rearrange("(c a) -> c a", a=1)).then_inc(params_in, 16)
            sp.dma_start(wr_c, wr_in).then_inc(params_in, 16)
            sp.dma_start(br_c, br_in.rearrange("(a n) -> a n", a=1).to_broadcast([C, 1])).then_inc(params_in, 16)
            for j in range(NB):
                sp.dma_start(b1c[:, j:j + 1], b1_in[j * C:(j + 1) * C].rearrange("(c a) -> c a", a=1)
                             ).then_inc(params_in, 16)
            sp.dma_start(w1_f, w1_in).then_inc(params_in, 16)
            sp.dma_start(w2_f[:, :, :], w2_in.rearrange("(n p) d -> p n d", p=C)).then_inc(params_in, 16)

            def phase1(n, b):
                if has(n + 2):
                    sp.wait_ge(split_ready, (n + 1) * NCH)
                    sp.dma_start(xb[b][:, :], x_v[bass.ds((n + 2) * C, C), :]).then_inc(x_in_s[b], 16)
                sp.wait_ge(y_copied, (n + 1) * NCH)
                sp.dma_start(y_dram[bass.ds(n * C, C), :], y16[b][:, :]).then_inc(y_saved[b], 16)

            pairs(sp, phase1, 1, n_img - 2, 0, n_img)

            def load(n, b):
                sp.dma_start(xb[b][:, :], x_v[bass.ds(n * C, C), :]).then_inc(xy_in[b], 16)
                sp.dma_start(y16[b][:, :], y_dram[bass.ds(n * C, C), :]).then_inc(xy_in[b], 16)

            for b in range(2):
                sp.wait_ge(y_saved[b], 16 * (n_img // 2))
            sp.wait_ge(bn_taken, n_img * NCH)
            load(0, 0)

            def phase2(n, b):
                if has(n):
                    sp.wait_ge(w_taken, n + 1)
                    sp.dma_start(w_dram[bass.ds(n, 1), :].rearrange("a (c t) -> (a c) t", t=T),
                                 wrow[:, :]).then_inc(w_saved, 16)
                    sp.wait_ge(w_saved, (n + 1) * 16)
                    w_n = w_dram[bass.ds(n, 1), :]
                    for s in range(SUB):
                        sp.dma_start(wse[s * CAND:(s + 1) * CAND, :],
                                     w_n[:, s * SLEN:(s + 1) * SLEN].to_broadcast([CAND, SLEN])
                                     ).then_inc(w_search_in, 16)
                    sp.dma_start(wk[:, :], w_n.rearrange("a (r t) -> (a r) t", t=MR_COLS)).then_inc(w_mask_in, 16)
                if has(n + 1):
                    sp.wait_ge(rms_ready, n + 2)
                    for q in range(2):
                        for s in range(2):
                            sp.dma_start(rows[32 * q + s:32 * q + s + 1, :].bitcast(f32)
                                         .rearrange("a (j p) -> a j p", p=TILE),
                                         rms[:, s, q, :].bitcast(f32)).then_inc(norm_rows_in, 16)
                if has(n - 1):
                    sp.wait_ge(out_ready, n * NCH)
                    sp.dma_start(out_v[bass.ds((n - 1) * C, C), :], yo[1 - b][:, :]).then_inc(out_saved[1 - b], 16)
                if has(n):
                    sp.wait_ge(gate_ready, n + 1)
                    for s in range(2):
                        sp.dma_start(rows[64 + s:65 + s, :].bitcast(f32)
                                     .rearrange("a (r t) -> a r t", t=MR_COLS),
                                     mks[:, s, :].bitcast(f32)).then_inc(gate_rows_in, 16)
                if has(n + 3):
                    if has(n + 1):
                        sp.wait_ge(base_ready, (n + 2) * NCH)
                    load(n + 3, 1 - b)

            pairs(sp, phase2, 1, n_img - 3, -2, n_img + 1)
            for b in range(2):
                sp.wait_ge(out_saved[b], 16 * (n_img // 2))

        @block.gpsimd
        def _(pool):
            nc.gpsimd.memset(wsel_h[:, :].bitcast(f32), 0.0).then_inc(prep_pool, 1)
            nc.gpsimd.memset(wsel_l[:, :].bitcast(f32), 0.0).then_inc(prep_pool, 1)
            pool.wait_ge(bound_ready, 1)
            nc.gpsimd.tensor_tensor(bound, bound2, half, ALU.pow).then_inc(bound_rooted, 1)
            pool.wait_ge(var_bn_ready, 1)
            nc.gpsimd.tensor_tensor(bn_r, bn_ve, kt[:, K_MHALF:K_MHALF + 1], ALU.pow).then_inc(bn_rooted, 1)

            def residual(n, b, c):
                pool.wait_ge(relu_ready, n * NCH + c + 1)
                nc.gpsimd.tensor_tensor(cut(xb[b], c), cut(xb[b], c), zr[(b + c) % 2][:, :],
                                        ALU.add).then_inc(x1_ready, 1)

            def low_part(n, b, c):
                pool.wait_ge(th_ready, n * NCH + c + 1)
                nc.gpsimd.tensor_tensor(cut(tl[b], c), tr[(b + c) % 2][:, :], cut(th[b], c).bitcast(f32),
                                        ALU.subtract).then_inc(tl_ready, 1)

            def phase2(n, b):
                for pos in range(POS + 1):
                    if pos == STAT_AT - 1 and has(n + 1):
                        pool.wait_ge(var_ready, n + 2)
                        nc.gpsimd.tensor_tensor(rm[:, 0, :], stw[:, 5, :], kt[0:TILE, K_MHALF:K_END],
                                                ALU.pow).then_inc(rstd_ready, 1)
                    if pos in RELU_AT and has(n + 2):
                        residual(n + 2, b, RELU_AT.index(pos))
                    if pos - 1 in NORM_AT and has(n + 1):
                        c = NORM_AT.index(pos - 1)
                        if has(n - 1) and c == 0:
                            pool.wait_ge(y_done, n * NCH)
                        low_part(n + 1, 1 - b, c)

            pairs(pool, phase2, *P2, -2, n_img + 1)

        @block.scalar
        def _(act):
            act.wait_ge(cw_centred, 1)
            nc.scalar.activation(cwa, cwc, ACT.Abs, accum_out=abs_sum).then_inc(abs_summed, 1)
            nc.scalar.activation(cws, cwc.rearrange("o (i t) -> o t i", t=TAPS),
                                 ACT.Sign).then_inc(cw_signed, 1)
            for t in range(TAPS):
                act.wait_ge(cw_transposed, t + 1)
                nc.scalar.activation(cwT[:, t, :], ps[:, t % 2, 0:C // 2].bitcast(bf16),
                                     ACT.Copy).then_inc(cw_ready, 1)

            def sign(n, b, c):
                g = n * NCH + c
                act.wait_ge(centred, g + 1)
                if c == 0:
                    if has(n - 2):
                        act.wait_ge(conv_done, (n - 1) * NCH)
                    if is_int(n) and n == 0:
                        act.wait_ge(border_clear, 2)
                bank = CEN_BANK + (b + c) % 2
                nc.scalar.activation(sg[b][:, 1 + c * ROWS:1 + (c + 1) * ROWS, 1:1 + SIDE],
                                     ps[:, bank, 0:T].rearrange("p (r w) -> p r w", w=SIDE),
                                     ACT.Sign).then_inc(signed, 1)

            for c in range(NCH):
                sign(0, 0, c)

            def phase1(n, b):
                for c in range(NCH):
                    act.wait_ge(conv_done, n * NCH + c + 1)
                    if c == 0 and has(n - 2):
                        act.wait_ge(y_saved[b], (n - b) * 8)
                        act.wait_ge(bn_taken, (n - 1) * NCH)
                    nc.scalar.activation(cut(y16[b], c), ps[:, CONV_BANK + (b + c) % 2, 0:T],
                                         ACT.Copy).then_inc(y_copied, 1)
                    if has(n + 1):
                        sign(n + 1, 1 - b, c)

            pairs(act, phase1, 3, n_img - 1, 0, n_img)
            act.wait_ge(coef_ready, 2)

            def phase2(n, b):
                for pos in range(POS + 1):
                    slot, j = divmod(pos, 2 * NB)
                    if pos < POS and j < NB and has(n):
                        g = n * NCH + slot
                        act.wait_ge(h_done, g * NB + j + 1)
                        if j == 0:
                            wait_count(act, y_done, g - 1)
                        nc.scalar.activation(hs[(b + slot) % 2][:, j, :], ps[:, H_BANK + j, 0:T],
                                             ACT.Gelu_apprx_tanh, bias=b1c[:, j:j + 1]).then_inc(gelu_done, 1)
                    if j == 2 * NB - 1 and (has(n) and slot > 0 or slot == 0 and has(n - 1)):
                        c = (slot - 1) % NCH
                        m, mb = (n, b) if slot > 0 else (n - 1, 1 - b)
                        act.wait_ge(y_done, m * NCH + c + 1)
                        if c == 0 and has(m - 2):
                            act.wait_ge(out_saved[mb], (m - mb) * 8)
                        nc.scalar.activation(cut(yo[mb], c), ps[:, Y_BANK, 0:T], ACT.Identity,
                                             bias=b2_c).then_inc(y_taken, 1)
                    if pos in RELU_AT and has(n + 2):
                        c = RELU_AT.index(pos)
                        g = (n + 2) * NCH + c
                        if c == 0:
                            act.wait_ge(xy_in[b], (n + 2 - b) * 16 + 32)
                        wait_count(act, x1_ready, g - 1)
                        nc.scalar.activation(zr[(b + c) % 2][:, :], cut(y16[b], c), ACT.Relu,
                                             bias=bn_t[:, :], scale=bn_s[:, :]).then_inc(relu_ready, 1)
                    if pos - 1 in NORM_AT and has(n + 1):
                        c = NORM_AT.index(pos - 1)
                        if c == 0 and has(n - 1):
                            act.wait_ge(y_done, n * NCH)
                        act.wait_ge(t_ready, (n + 1) * NCH + c + 1)
                        nc.scalar.activation(cut(th[1 - b], c), tr[(1 - b + c) % 2][:, :],
                                             ACT.Copy).then_inc(th_ready, 1)

            pairs(act, phase2, 3, n_img - 3, -2, n_img + 1)

        @block.vector
        def _(dve):
            done = [0]

            def link(ins):
                done[0] += 1
                ins.then_inc(prep, 1)
                dve.wait_ge(prep, done[0])

            V = nc.vector
            for b in range(2):
                V.memset(sg[b], 0.0).then_inc(border_clear, 1)
            dve.wait_ge(params_in, 16 * N_PARAMS)
            V.tensor_copy(centre_r[:, :], kt[:, K_CEN:K_CEN + C]).then_inc(tables_ready, 1)

            def split(n, b, c):
                g = n * NCH + c
                if c == 0:
                    dve.wait_ge(x_in_s[b], (n - b) * 8 + 16)
                wait_count(dve, centred, g - 1)
                V.tensor_copy(xh[(b + c) % 2][:, :], cut(xb[b], c)).then_inc(xh_ready, 1)

            def split_low(n, b, c):
                dve.wait_ge(xh_ready, n * NCH + c + 1)
                V.tensor_tensor(xl[(b + c) % 2][:, :], cut(xb[b], c), xh[(b + c) % 2][:, :].bitcast(f32),
                                ALU.subtract).then_inc(split_ready, 1)

            link(V.tensor_reduce(wmean, cw.rearrange("o (i t) -> o t i", t=TAPS), AX.X, ALU.add))
            link(V.tensor_scalar(wmean, wmean, 1.0 / C, None, ALU.mult))
            cw3 = cw.rearrange("o (i t) -> o i t", t=TAPS)
            cwc3 = cwc.rearrange("o (i t) -> o i t", t=TAPS)
            for t in range(TAPS):
                last = V.tensor_scalar(cwc3[:, :, t], cw3[:, :, t], wmean[:, t:t + 1], -1.0, ALU.subtract, ALU.max)
            link(last)
            V.tensor_scalar(cwc, cwc, 1.0, None, ALU.min).then_inc(cw_centred, 1)
            V.tensor_copy(ident_b[:, :], ident).then_inc(tables_ready, 1)
            V.tensor_tensor(wr2, wr_c, wr_c, ALU.mult).then_inc(wr2_ready, 1)
            V.memset(half, 0.5)
            V.tensor_copy(w1_h[:, :], w1_f)
            V.tensor_copy(ones_r[:, :], kt[:, K_ONES:K_ONES + C])
            dve.wait_ge(prep_pool, 2)
            link(V.tensor_copy(wsel_h[:, C:C + 1], wr_c))
            V.tensor_tensor(w1_l[:, :], w1_f, w1_h[:, :].bitcast(f32), ALU.subtract)
            link(V.tensor_tensor(wsel_l[:, C:C + 1], wr_c, wsel_h[:, C:C + 1].bitcast(f32), ALU.subtract))
            dve.wait_ge(wr2_summed, 1)
            V.tensor_scalar(bound2, ps[:, BC0, 0:1], float(C), 1e-30, ALU.mult, ALU.add).then_inc(bound_ready, 1)
            link(V.scalar_tensor_tensor(lo_c, br_c, -1.0, br_c, ALU.mult, ALU.max))
            dve.wait_ge(bound_rooted, 1)
            link(V.tensor_tensor(bound, bound, lo_c, ALU.add))
            link(V.tensor_scalar(bound.bitcast(i32), bound.bitcast(i32), 0x7F800000, None, ALU.bitwise_and))
            link(V.tensor_scalar(neg_b[:, :], bound, -2.0, None, ALU.mult))
            for r in range(ROUNDS):
                last = V.tensor_scalar(steps[:, r:r + 1], neg_b[:, :], -2.0 / CAND ** (r + 1), None, ALU.mult)
            link(last)
            link(V.tensor_scalar(candc[:, :], steps[:, :], kt[:, K_CIDX:K_CIDX + 1], None, ALU.mult))
            link(V.tensor_tensor(cand0[:, :], neg_b[:, :], candc[:, 0:1], ALU.add))

            for c in range(NCH):
                split(0, 0, c)
                split_low(0, 0, c)

            def phase1(n, b):
                for c in range(NCH):
                    g = n * NCH + c
                    if has(n + 1):
                        split(n + 1, 1 - b, c)
                        split_low(n + 1, 1 - b, c)
                    dve.wait_ge(y_copied, g + 1)
                    V.bn_stats(bnst[:, g, :] if is_int(g) else bnst[:, bass.ds(g, 1), :],
                               cut(y16[b], c)).then_inc(bn_taken, 1)

            pairs(dve, phase1, *P1, 0, n_img)

            dve.wait_ge(bn_taken, n_img * NCH)
            link(V.bn_aggr(bn_mv, bnst[:, :, :]))
            dve.wait_ge(abs_summed, 1)
            link(V.tensor_scalar(alpha[:, :], abs_sum, 1.0 / (C * TAPS), None, ALU.mult))
            link(V.scalar_tensor_tensor(mean_y, bn_mv[:, 0:1], alpha[:, :], cb_c, ALU.mult, ALU.add))
            link(V.tensor_scalar(bn_ve, bn_mv[:, 1:2], alpha[:, :], alpha[:, :], ALU.mult, ALU.mult))
            V.tensor_scalar(bn_ve, bn_ve, EPS, None, ALU.add).then_inc(var_bn_ready, 1)
            link(V.tensor_tensor(bias_d, cb_c, mean_y, ALU.subtract))
            dve.wait_ge(bn_rooted, 1)
            link(V.tensor_tensor(bn_r, bn_r, gamma_c, ALU.mult))
            V.tensor_tensor(bn_s[:, :], bn_r, alpha[:, :], ALU.mult).then_inc(coef_ready, 1)
            V.scalar_tensor_tensor(bn_t[:, :], bias_d, bn_r, beta_c, ALU.mult, ALU.add).then_inc(coef_ready, 1)

            def tile_stats(m, c):
                dve.wait_ge(transposed, m * NCH + c + 1)
                for i in range(TPG):
                    last = V.bn_stats(st[:, c * TPG + i, :], ps[0:TILE, T_BANK, i * C:(i + 1) * C])
                last.then_inc(stats_taken, 1)

            STAT_STEPS = 5
            mean2, dif, m2sum, sq, var_c, ve_c = (stw[:, i, :] for i in range(6))

            def link_stat(ins, m, j):
                ins.then_inc(stat_step, 1)
                dve.wait_ge(stat_step, m * STAT_STEPS + j)

            def token_variance(m):
                dve.wait_ge(stats_taken, (m + 1) * NCH)
                V.tensor_tensor(mean2, st[:, :, 1], st[:, :, 4], ALU.add)
                link_stat(V.tensor_tensor(dif, st[:, :, 1], st[:, :, 4], ALU.subtract), m, 1)
                V.tensor_tensor(m2sum, st[:, :, 2], st[:, :, 5], ALU.add)
                link_stat(V.tensor_tensor(sq, dif, dif, ALU.mult), m, 2)
                link_stat(V.scalar_tensor_tensor(var_c, sq, C / 4.0, m2sum, ALU.mult, ALU.add), m, 3)
                V.tensor_scalar(ve_c, var_c, 1.0 / C, EPS, ALU.mult, ALU.add).then_inc(var_ready, 1)

            def mean_over_std(m):
                dve.wait_ge(rstd_ready, m + 1)
                V.scalar_tensor_tensor(rm[:, 1, :], mean2, 0.5, rm[:, 0, :], ALU.mult, ALU.mult).then_inc(mr_ready, 1)

            def split_stats(m):
                dve.wait_ge(stat_rows, m + 1)
                src = ps[0:NT, T_BANK, 0:2 * C].rearrange("j (q p) -> j q p", q=2)[:, :, 0:TILE]
                link_stat(V.tensor_copy(rms[:, 0, :, :], src), m, 4)
                V.tensor_tensor(rms[:, 1, :, :], src, rms[:, 0, :, :].bitcast(f32),
                                ALU.subtract).then_inc(rms_ready, 1)
                V.tensor_copy(stw[0:1, 3, 0:1], stw[0:1, 2, 0:1]).then_inc(stat_step, 1)

            def normalise(m, b, c):
                g = m * NCH + c
                ring = (b + c) % 2
                dve.wait_ge(bc_stats, 2 * g + 1)
                V.tensor_tensor(ur[ring][:, :], cut(xb[b], c), ps[:, BC0, 0:T], ALU.mult).then_inc(u_ready, 1)
                dve.wait_ge(bc_stats, 2 * g + 2)
                dve.wait_ge(u_ready, g + 1)
                wait_count(dve, th_ready, g - 1)
                wait_count(dve, tl_ready, g - 1)
                V.tensor_tensor(tr[ring][:, :], ur[ring][:, :], ps[:, BC1, 0:T], ALU.subtract).then_inc(t_ready, 1)
                dve.wait_ge(t_ready, g + 1)
                V.tensor_tensor(cut(base[b], c), cut(xb[b], c), tr[ring][:, :], ALU.add).then_inc(base_ready, 1)

            def take_router(n):
                dve.wait_ge(w_done, n + 1)
                if has(n - 1):
                    dve.wait_ge(w_saved, n * 16)
                V.tensor_scalar(wrow[:, :], ps[0:NCH, T_BANK, 0:T], br_c[0:NCH, :], None,
                                ALU.add).then_inc(w_taken, 1)

            SEARCH_STEPS = 2 * ROUNDS - 1

            def count_above(n, r):
                if r == 0:
                    dve.wait_ge(w_search_in, (n + 1) * 16 * SUB)
                else:
                    dve.wait_ge(search_step, n * SEARCH_STEPS + 2 * r)
                V.tensor_scalar(junk[:, :], wse[:, :], cand0[:, :] if r == 0 else cand_c, None, ALU.is_ge, ALU.add,
                                accum_out=cnt_c).then_inc(search_dve, 1)

            def flag_candidates(n, r):
                dve.wait_ge(search_pe, n * 2 * ROUNDS + 2 * r + 1)
                V.tensor_scalar(flag_c, cnt_ps, float(TOP), None, ALU.is_ge).then_inc(search_dve, 1)

            def narrow(n, r):
                dve.wait_ge(search_pe, n * 2 * ROUNDS + 2 * r + 2)
                V.scalar_tensor_tensor(lo_c, idx_ps, steps[:, r:r + 1], neg_b[:, :] if r == 0 else lo_c,
                                       ALU.mult, ALU.add).then_inc(search_step, 1)
                dve.wait_ge(search_step, n * SEARCH_STEPS + 2 * r + 1)
                if r + 1 < ROUNDS:
                    V.tensor_tensor(cand_c, lo_c, candc[:, r + 1:r + 2], ALU.add).then_inc(search_step, 1)

            above, at_least, ties, keep, chosen, gate = (mk[:, i, :] for i in range(6))
            R = slice(0, MR_ROWS)
            MASK_STEPS = 7

            def link_mask(ins, n, j):
                ins.then_inc(mask_step, 1)
                dve.wait_ge(mask_step, n * MASK_STEPS + j)

            def find_ties(n):
                dve.wait_ge(w_mask_in, (n + 1) * 16)
                V.tensor_scalar(at_least, wk[:, :], lo_c[R, :], 0.0, ALU.subtract, ALU.is_ge)
                link_mask(V.tensor_scalar(above, wk[:, :], lo_c[R, :], steps[R, ROUNDS - 1:ROUNDS],
                                          ALU.subtract, ALU.is_ge), n, 1)
                link_mask(V.tensor_tensor(ties, at_least, above, ALU.subtract), n, 2)
                V.tensor_reduce(rowg_c[R, :], above, AX.X, ALU.add)
                V.tensor_reduce(rowe_c[R, :], ties, AX.X, ALU.add).then_inc(ties_ready, 1)

            def copy_ties(n):
                dve.wait_ge(ties_t, n + 1)
                V.tensor_copy(et[:, :], ps[0:MR_COLS, T_BANK, 0:MR_ROWS])
                V.tensor_copy(off_c[R, :], off_ps).then_inc(ties_copied, 1)

            def gates(n):
                dve.wait_ge(ties_scanned, n + 1)
                dve.wait_ge(ties_copied, n + 1)
                link_mask(V.tensor_scalar(keep, ps[R, T_BANK, C:C + MR_COLS], off_c[R, :], float(TOP),
                                          ALU.add, ALU.is_le), n, 3)
                link_mask(V.tensor_tensor(keep, keep, ties, ALU.mult), n, 4)
                link_mask(V.tensor_tensor(chosen, above, keep, ALU.add), n, 5)
                link_mask(V.tensor_tensor(gate, chosen, wk[:, :], ALU.mult), n, 6)
                link_mask(V.tensor_copy(mks[:, 0, :], gate), n, 7)
                V.tensor_tensor(mks[:, 1, :], gate, mks[:, 0, :].bitcast(f32), ALU.subtract).then_inc(gate_ready, 1)

            def gate_and_sum(m, b, c):
                g = m * NCH + c
                dve.wait_ge(bc_gate, g + 1)
                dve.wait_ge(y_taken, g + 1)
                V.tensor_tensor(cut(yo[b], c), cut(yo[b], c), ps[:, BC1, 0:T], ALU.mult).then_inc(gated, 1)
                dve.wait_ge(gated, g + 1)
                dve.wait_ge(base_ready, g + 1)
                V.tensor_tensor(cut(yo[b], c), cut(yo[b], c), cut(base[b], c), ALU.add).then_inc(out_ready, 1)

            def phase2(n, b):
                for pos in range(POS):
                    if pos == WROW_AT + 1 and has(n):
                        take_router(n)
                    if pos + 1 in COUNT_AT and has(n):
                        count_above(n, COUNT_AT.index(pos + 1))
                    if pos in COUNT_AT and has(n):
                        flag_candidates(n, COUNT_AT.index(pos))
                    if pos in INDEX_AT and has(n):
                        narrow(n, INDEX_AT.index(pos))
                    if pos == INDEX_AT[-1] + 1 and has(n):
                        find_ties(n)
                    if pos == MASK_AT and has(n):
                        copy_ties(n)
                    if pos == SCAN_AT and has(n):
                        gates(n)
                    if pos in TRANSPOSE_AT and has(n + 1):
                        tile_stats(n + 1, TRANSPOSE_AT.index(pos))
                    if pos == TRANSPOSE_AT[-1] + 1 and has(n + 1):
                        token_variance(n + 1)
                    if pos == STAT_AT - 1 and has(n + 1):
                        mean_over_std(n + 1)
                    if pos == STAT_AT and has(n + 1):
                        split_stats(n + 1)
                    if pos in OUT_AT and has(n - 1):
                        gate_and_sum(n - 1, 1 - b, OUT_AT.index(pos))
                    if pos in NORM_AT and has(n + 1):
                        normalise(n + 1, 1 - b, NORM_AT.index(pos))

            pairs(dve, phase2, *P2, -1, n_img + 1)

        @block.tensor
        def _(pe):
            M = nc.tensor.matmul
            pe.wait_ge(wr2_ready, 1)
            M(ps[:, BC0, 0:1], kt[:, K_ONES:K_ONES + C], wr2, start=True, stop=True).then_inc(wr2_summed, 1)
            pe.wait_ge(tables_ready, 2)
            pe.wait_ge(cw_signed, 1)
            for t in range(TAPS):
                wait_count(pe, cw_ready, t - 1)
                nc.tensor.transpose(ps[:, t % 2, 0:C // 2].bitcast(bf16), cws[:, t, :],
                                    ident_b[:, :]).then_inc(cw_transposed, 1)
            pe.wait_ge(cw_ready, TAPS)

            def centre(n, b, c):
                g = n * NCH + c
                pe.wait_ge(split_ready, g + 1)
                wait_count(pe, signed, g - 1)
                bank = ps[:, CEN_BANK + (b + c) % 2, 0:T]
                M(bank, centre_r[:, :], xh[(b + c) % 2][:, :], start=True, stop=False)
                M(bank, centre_r[:, :], xl[(b + c) % 2][:, :], start=False, stop=True).then_inc(centred, 1)

            def conv(n, b, c):
                g = n * NCH + c
                pe.wait_ge(signed, n * NCH + min(c + 2, NCH))
                wait_count(pe, y_copied, g - 1)
                bank = ps[:, CONV_BANK + (b + c) % 2, 0:T].rearrange("p (r w) -> p r w", w=SIDE)
                for t in range(TAPS):
                    dy, dx = divmod(t, 3)
                    last = M(bank, cwT[:, t, :], sg[b][:, c * ROWS + dy:c * ROWS + dy + ROWS, dx:dx + SIDE],
                             start=t == 0, stop=t == TAPS - 1)
                last.then_inc(conv_done, 1)

            for c in range(NCH):
                centre(0, 0, c)

            def phase1(n, b):
                for c in range(NCH):
                    conv(n, b, c)
                    if has(n + 1):
                        centre(n + 1, 1 - b, c)

            pairs(pe, phase1, *P1, 0, n_img)
            pe.wait_ge(y_copied, n_img * NCH)
            pe.wait_ge(bn_taken, n_img * NCH)

            def transposes(m, b, c, n):
                pe.wait_ge(x1_ready, m * NCH + c + 1)
                if c == 0:
                    if has(n - 1):
                        pe.wait_ge(gate_ready, n)
                else:
                    pe.wait_ge(stats_taken, m * NCH + c)
                if c and TRANSPOSE_AT[c - 1] < WROW_AT < TRANSPOSE_AT[c] and has(n):
                    pe.wait_ge(w_taken, n + 1)
                for i in range(TPG):
                    lo = c * T + i * TILE
                    last = nc.tensor.transpose(ps[0:TILE, T_BANK, i * C:(i + 1) * C], xb[b][:, lo:lo + TILE], ident)
                last.then_inc(transposed, 1)

            def router(n, b):
                pe.wait_ge(tl_ready, (n + 1) * NCH)
                if has(n + 1):
                    done = sum(p < WROW_AT for p in TRANSPOSE_AT)
                    pe.wait_ge(stats_taken, (n + 1) * NCH + done)
                bank = ps[:, T_BANK, 0:T]
                for c in range(NCH):
                    for i, (w, t) in enumerate(((wsel_h, th), (wsel_h, tl), (wsel_l, th))):
                        last = M(bank, w[:, C - c:2 * C - c], cut(t[b], c), start=c == 0 and i == 0,
                                 stop=c == NCH - 1 and i == 2)
                last.then_inc(w_done, 1)

            def rows_of_stats(m, n):
                pe.wait_ge(mr_ready, m + 1)
                if has(n):
                    done = sum(p <= STAT_AT for p in COUNT_AT) + sum(p < STAT_AT for p in INDEX_AT)
                    pe.wait_ge(search_dve, n * 2 * ROUNDS + done + 1)
                for q in range(2):
                    last = nc.tensor.transpose(ps[0:NT, T_BANK, q * C:q * C + TILE], rm[:, q, :],
                                               ident[0:TILE, 0:TILE])
                last.then_inc(stat_rows, 1)

            def spread_stats(m, b, c, n, pos):
                g = m * NCH + c
                if c == 0:
                    pe.wait_ge(norm_rows_in, (m + 1) * 64)
                wait_count(pe, u_ready, g)
                M(ps[:, BC0, 0:T], ones_r[0:2, :], cut(rows[0:2, :], c), start=True, stop=True).then_inc(bc_stats, 1)
                wait_count(pe, t_ready, g)
                if has(n - 1):
                    pe.wait_ge(gated, (n - 1) * NCH + sum(p <= pos for p in OUT_AT))
                M(ps[:, BC1, 0:T], ones_r[32:34, :], cut(rows[32:34, :], c), start=True, stop=True).then_inc(bc_stats, 1)

            def spread_gates(m, b, c, n, pos):
                g = m * NCH + c
                if c == 0:
                    pe.wait_ge(gate_rows_in, (m + 1) * 32)
                if c:
                    pe.wait_ge(gated, g)
                if has(n + 1):
                    pe.wait_ge(t_ready, (n + 1) * NCH + sum(p < pos for p in NORM_AT))
                else:
                    pe.wait_ge(t_ready, (n if has(n) else n_img) * NCH + (NCH if has(n) else 0))
                M(ps[:, BC1, 0:T], ones_r[64:66, :], cut(rows[64:66, :], c), start=True, stop=True).then_inc(bc_gate, 1)

            def hidden(n, b, c, j):
                g = n * NCH + c
                if j == 0:
                    pe.wait_ge(tl_ready, g + 1)
                wait_count(pe, gelu_done, (g - 1) * NB + j + 1)
                bank = ps[:, H_BANK + j, 0:T]
                blk = slice(j * C, (j + 1) * C)
                M(bank, w1_h[:, blk], cut(th[b], c), start=True, stop=False)
                M(bank, w1_h[:, blk], cut(tl[b], c), start=False, stop=False)
                M(bank, w1_l[:, blk], cut(th[b], c), start=False, stop=True).then_inc(h_done, 1)

            def output(n, b, c, j):
                g = n * NCH + c
                pe.wait_ge(gelu_done, g * NB + j + 1)
                if j == 0:
                    wait_count(pe, y_taken, g)
                last = M(ps[:, Y_BANK, 0:T], w2_f[:, j, :], hs[(b + c) % 2][:, j, :], start=j == 0, stop=j == NB - 1)
                if j == NB - 1:
                    last.then_inc(y_done, 1)

            def count_candidates(n, r):
                pe.wait_ge(search_dve, n * 2 * ROUNDS + 2 * r + 1)
                if r == 0 and has(n + 1):
                    pe.wait_ge(stats_taken, (n + 2) * NCH)
                M(cnt_ps, kt[:, K_SAME:K_SAME + C], cnt_c, start=True, stop=True).then_inc(search_pe, 1)

            def choose_candidate(n, r):
                pe.wait_ge(search_dve, n * 2 * ROUNDS + 2 * r + 2)
                if r == 0 and has(n + 1):
                    pe.wait_ge(rms_ready, n + 2)
                M(idx_ps, kt[:, K_FLAG:K_FLAG + C], flag_c, start=True, stop=True).then_inc(search_pe, 1)

            def transpose_ties(n):
                pe.wait_ge(ties_ready, n + 1)
                R = slice(0, MR_ROWS)
                nc.tensor.transpose(ps[0:MR_COLS, T_BANK, 0:MR_ROWS], ties_sb, ident[R, R])
                M(off_ps, kt[R, K_ONES:K_ONES + MR_ROWS], rowg_c[R, :], start=True, stop=False)
                M(off_ps, kt[R, K_STRI:K_STRI + MR_ROWS], rowe_c[R, :], start=False, stop=True).then_inc(ties_t, 1)

            def scan_ties(n):
                pe.wait_ge(ties_copied, n + 1)
                M(ps[0:MR_ROWS, T_BANK, C:C + MR_COLS], et[:, :], kt[0:MR_COLS, K_TRIU:K_TRIU + MR_COLS],
                  start=True, stop=True).then_inc(ties_scanned, 1)

            def phase2(n, b):
                for pos in range(POS):
                    c, j = divmod(pos, 2 * NB)
                    if j < NB and has(n):
                        hidden(n, b, c, j)
                    if j >= NB and c > 0 and has(n):
                        output(n, b, c - 1, j - NB)
                    if j >= NB and c == 0 and has(n - 1):
                        output(n - 1, 1 - b, NCH - 1, j - NB)
                    if pos in TRANSPOSE_AT and has(n + 1):
                        transposes(n + 1, 1 - b, TRANSPOSE_AT.index(pos), n)
                    if pos == WROW_AT and has(n):
                        router(n, b)
                    if pos in COUNT_AT and has(n):
                        count_candidates(n, COUNT_AT.index(pos))
                    if pos in INDEX_AT and has(n):
                        choose_candidate(n, INDEX_AT.index(pos))
                    if pos == MASK_AT and has(n):
                        transpose_ties(n)
                    if pos == SCAN_AT and has(n):
                        scan_ties(n)
                    if pos == STAT_AT and has(n + 1):
                        rows_of_stats(n + 1, n)
                    if pos in OUT_AT and has(n - 1):
                        spread_gates(n - 1, 1 - b, OUT_AT.index(pos), n, pos)
                    if pos in NORM_AT and has(n + 1):
                        spread_stats(n + 1, 1 - b, NORM_AT.index(pos), n, pos)

            pairs(pe, phase2, *P2, -1, n_img + 1)


N_PARAMS = 14
_INS = ["x", "L0_conv_w", "L0_conv_b", "L0_conv_gamma", "L0_conv_beta", "L0_ffn_wr", "L0_ffn_br",
        "L0_ffn_w1", "L0_ffn_b1", "L0_ffn_w2", "L0_ffn_b2"]


def kernel(**inputs):
    import concourse.bacc as _bacc
    from concourse.bass_utils import run_bass_kernel_spmd as _run

    nc = _bacc.Bacc("TRN2", target_bir_lowering=False, num_devices=1)
    arrays = {"consts": constants()}
    for name in _INS:
        arrays[name] = np.ascontiguousarray(inputs[name])
    args = [nc.dram_tensor(name, a.shape, mybir.dt.from_np(a.dtype), kind="ExternalInput").ap()
            for name, a in arrays.items()]
    shape = arrays["x"].shape
    args.append(nc.dram_tensor("result", shape, mybir.dt.float32, kind="ExternalOutput").ap())
    block_kernel(nc, *args, shape[0])
    r = _run(nc, [arrays], core_ids=[0])
    return r.results[0]["result"]
```

```python
import numpy as np
import concourse.bass as bass
from concourse import mybir
from contextlib import ExitStack

C = 128
SIDE = 56
TOK = SIDE * SIDE
ROWS = 8
T = ROWS * SIDE
NCH = TOK // T
TAPS = 9
PAD = SIDE + 2
TILE = 112
NT = TOK // TILE
TPG = T // TILE
HID = 512
NB = HID // C
TOP = max(1, int(0.5 * TOK)) - 1
CAND = 16
SUB = C // CAND
SLEN = TOK // SUB
ROUNDS = 8
MR_ROWS, MR_COLS = 98, 32
EPS = 1e-5

K_ID, K_CEN, K_SAME, K_FLAG, K_STRI, K_TRIU, K_ONES, K_CIDX, K_MHALF, K_END = (
    0, 128, 256, 384, 512, 640, 672, 800, 801, 801 + NT)


def constants():
    t = np.zeros((C, K_END), np.float32)
    p, q = np.arange(C)[:, None], np.arange(C)[None, :]
    t[:, K_ID:K_ID + C] = p == q
    t[:, K_CEN:K_CEN + C] = (p == q) - 1.0 / C
    t[:, K_SAME:K_SAME + C] = p % CAND == q % CAND
    t[:, K_FLAG:K_FLAG + C] = (p >= 1) & (p < CAND)
    t[:, K_STRI:K_STRI + C] = p < q
    t[:, K_TRIU:K_TRIU + MR_COLS] = p <= q[:, :MR_COLS]
    t[:, K_ONES:K_ONES + C] = 1.0
    t[:, K_CIDX] = np.arange(C) % CAND
    t[:, K_MHALF:K_END] = -0.5
    return t


POS = 2 * NB * NCH
TRANSPOSE_AT = [0, 2, 6, 8, 10, 12, 14]
WROW_AT = 4
VAR_AT = 15
STAT_AT = 22
NORM_AT = [29, 33, 37, 41, 45, 49, 53]
OUT_AT = [5, 8, 11, 15, 19, 24, 27]
COUNT_AT = [15, 21, 25, 29, 34, 38, 42, 47]
INDEX_AT = [17, 23, 27, 31, 36, 40, 44, 49]
MASK_AT = 53
SCAN_AT = 55
RELU_AT = [12, 18, 24, 30, 36, 42, 48]
SPLIT = {1: "dve", 3: "pool"}


def block_kernel(nc, consts, x_in, cw_in, cb_in, gamma_in, beta_in, wr_in, br_in, w1_in, b1_in,
                 w2_in, b2_in, out, n_img):
    f32, f32r = mybir.dt.float32, mybir.dt.float32r
    bf16, f16, i32 = mybir.dt.bfloat16, mybir.dt.float16, mybir.dt.int32
    ALU = mybir.AluOpType
    ACT = mybir.ActivationFunctionType
    AX = mybir.AxisListType

    x_v = x_in.rearrange("b c h w -> (b c) (h w)")
    out_v = out.rearrange("b c h w -> (b c) (h w)")
    y_dram = nc.dram_tensor("y_int", [n_img * C, TOK], f16).ap()
    w_dram = nc.dram_tensor("w_row", [n_img, TOK], f32).ap()

    with ExitStack() as ctx:
        def sb(name, shape, dt):
            return ctx.enter_context(nc.sbuf_tensor(name, shape, dt))

        def sem(name):
            return ctx.enter_context(nc.semaphore(name))

        kt = sb("kt", [C, K_END], f32)
        ident = kt[:, K_ID:K_ID + C]
        centre_r = sb("centre_r", [C, C], f32r)
        ones_r = sb("ones_r", [C, C], f32r)
        cwT = sb("cwT", [C, TAPS, C], bf16)
        w1_h = sb("w1_h", [C, HID], f32r)
        w1_l = sb("w1_l", [C, HID], f32r)
        w2_f = sb("w2_f", [C, NB, C], f32)
        w2_h = sb("w2_h", [C, NB, C], f32r)
        w2_l = sb("w2_l", [C, NB, C], f32r)
        b1c = sb("b1c", [C, NB], f32)
        cols = sb("cols", [C, 8], f32)
        cb_c, gamma_c, beta_c, b2_c, wr_c, br_c = (cols[:, i:i + 1] for i in range(6))
        wsel_h = sb("wsel_h", [C, 2 * C], f32r)
        wsel_l = sb("wsel_l", [C, 2 * C], f32r)
        sm = sb("sm", [C, 32], f32)
        (wr2, bound2, bound, half, abs_sum, bn_ve, bn_r, mean_y, bias_d) = (sm[:, i:i + 1] for i in range(9))
        wmean = sm[:, 16:16 + TAPS]
        bn_mv = sm[:, 26:28]
        ident_b = sb("ident_b", [C, C], bf16)
        steps = sb("steps", [C, ROUNDS], f32)
        candc = sb("candc", [C, ROUNDS], f32)
        neg_b = sb("neg_b", [C, 1], f32)
        cand0 = sb("cand0", [C, 1], f32)
        alpha = sb("alpha", [C, 1], f32)
        bn_s = sb("bn_s", [C, 1], f32)
        bn_t = sb("bn_t", [C, 1], f32)

        xb = [sb(f"xb{b}", [C, TOK], f32) for b in range(2)]
        y16 = [sb(f"y16{b}", [C, TOK], f16) for b in range(2)]
        base = [sb(f"base{b}", [C, TOK], f32) for b in range(2)]
        yo = [sb(f"yo{b}", [C, TOK], f32) for b in range(2)]
        th = sb("th", [C, TOK], f32r)
        tl = sb("tl", [C, TOK], f32r)
        sg = [yo[b][:, 0:PAD * PAD // 2].bitcast(bf16).rearrange("p (r w) -> p r w", w=PAD) for b in range(2)]
        bnst = base[0][:, 0:n_img * NCH * 6].rearrange("p (g s) -> p g s", s=6)

        xh = [th[:, b * T:(b + 1) * T] for b in range(2)]
        xl = [tl[:, b * T:(b + 1) * T] for b in range(2)]
        zr = [sb(f"zr{b}", [C, T], f32) for b in range(2)]
        ur = [sb(f"ur{b}", [C, T], f32) for b in range(2)]
        tr = [sb(f"tr{b}", [C, T], f32) for b in range(2)]
        hs = [sb(f"hs{b}", [C, NB, T], f32) for b in range(2)]
        hh = [sb(f"hh{b}", [C, len(SPLIT), T], f32r) for b in range(2)]
        hl = [sb(f"hl{b}", [C, len(SPLIT), T], f32r) for b in range(2)]
        cw, cwc = (h[:, :, :].rearrange("p a b -> p (a b)")[:, 0:C * TAPS] for h in hs)
        cwa = base[1][:, 0:C * TAPS]
        cws = base[1][:, C * TAPS:C * TAPS * 3 // 2].bitcast(bf16).rearrange("o (t i) -> o t i", i=C)
        w1_f = base[1][:, 2 * C * TAPS:2 * C * TAPS + HID]
        rows = sb("rows", [C, TOK], f32r)
        st = sb("st", [TILE, NT, 6], f32)
        stw = sb("stw", [TILE, 6, NT], f32)
        rm = sb("rm", [TILE, 2, NT], f32)
        rms = sb("rms", [NT, 2, 2, TILE], f32r)
        wrow = sb("wrow", [NCH, T], f32)
        wse = sb("wse", [C, SLEN], f32)
        junk = sb("junk", [C, SLEN], bf16)
        wk = sb("wk", [MR_ROWS, MR_COLS], f32)
        mk = sb("mk", [MR_ROWS, 8, MR_COLS], f32)
        mks = sb("mks", [MR_ROWS, 2, MR_COLS], f32r)
        et = sb("et", [MR_COLS, MR_ROWS], f32)
        srch = sb("srch", [C, 8], f32)
        lo_c, cand_c, rowg_c, rowe_c, off_c = (srch[:, i:i + 1] for i in range(5))
        srch16 = sb("srch16", [C, 2], f16)
        cnt_c, flag_c = srch16[:, 0:1], srch16[:, 1:2]
        same_b = sb("same_b", [C, C], f16)
        flag_b = sb("flag_b", [C, C], f16)

        ps = ctx.enter_context(nc.psum_tensor("ps", [C, 8, 512], f32))
        H_BANK, Y_BANK, T_BANK, BC0, BC1 = 0, 4, 5, 6, 7
        CEN_BANK, CONV_BANK = 0, 2
        ties_sb = mk[:, 2, :]
        cnt_ps = ps[:, T_BANK, 0:1]
        idx_ps = ps[:, T_BANK, 1:2]
        off_ps = ps[0:MR_ROWS, T_BANK, T:T + 1]

        params_in = sem("params_in")
        prep = sem("prep")
        prep_pool = sem("prep_pool")
        wr2_ready = sem("wr2_ready")
        wr2_summed = sem("wr2_summed")
        bound_ready = sem("bound_ready")
        bound_rooted = sem("bound_rooted")
        cw_centred = sem("cw_centred")
        abs_summed = sem("abs_summed")
        cw_signed = sem("cw_signed")
        cw_transposed = sem("cw_transposed")
        tables_ready = sem("tables_ready")
        var_bn_ready = sem("var_bn_ready")
        bn_rooted = sem("bn_rooted")
        cw_ready = sem("cw_ready")
        border_clear = sem("border_clear")
        x_in_s = [sem(f"x_in{b}") for b in range(2)]
        xh_ready = sem("xh_ready")
        split_ready = sem("split_ready")
        centred = sem("centred")
        signed = sem("signed")
        conv_done = sem("conv_done")
        y_copied = sem("y_copied")
        bn_taken = sem("bn_taken")
        y_saved = [sem(f"y_saved{b}") for b in range(2)]
        coef_ready = sem("coef_ready")
        xy_in = [sem(f"xy_in{b}") for b in range(2)]
        relu_ready = sem("relu_ready")
        x1_ready = sem("x1_ready")
        transposed = sem("transposed")
        stats_taken = sem("stats_taken")
        stat_step = sem("stat_step")
        var_ready = sem("var_ready")
        rstd_ready = sem("rstd_ready")
        mr_ready = sem("mr_ready")
        stat_rows = sem("stat_rows")
        rms_h = sem("rms_h")
        rms_ready = sem("rms_ready")
        norm_rows_in = sem("norm_rows_in")
        bc_stats = sem("bc_stats")
        u_ready = sem("u_ready")
        t_ready = sem("t_ready")
        base_ready = sem("base_ready")
        th_ready = sem("th_ready")
        tl_ready = sem("tl_ready")
        w_done = sem("w_done")
        w_taken = sem("w_taken")
        w_saved = sem("w_saved")
        w_search_in = sem("w_search_in")
        w_mask_in = sem("w_mask_in")
        search_dve = sem("search_dve")
        search_pe = sem("search_pe")
        search_step = sem("search_step")
        mask_step = sem("mask_step")
        ties_ready = sem("ties_ready")
        ties_t = sem("ties_t")
        ties_copied = sem("ties_copied")
        ties_scanned = sem("ties_scanned")
        gate_ready = sem("gate_ready")
        gate_rows_in = sem("gate_rows_in")
        bc_gate = sem("bc_gate")
        h_done = sem("h_done")
        gelu_done = sem("gelu_done")
        hh_ready = sem("hh_ready")
        hl_ready = {e: sem(f"hl_ready_{e}") for e in set(SPLIT.values())}
        y_done = sem("y_done")
        y_taken = sem("y_taken")
        gated = sem("gated")
        out_ready = sem("out_ready")
        out_saved = [sem(f"out_saved{b}") for b in range(2)]

        def wait_count(eng, semaphore, value):
            if not (isinstance(value, int) and value <= 0):
                eng.wait_ge(semaphore, value)

        def pairs(eng, body, first, last, lo, hi):
            for n in range(lo, first):
                body(n, n % 2)
            turns = (last - first) // 2
            with eng.Fori(0, turns) as k:
                body(k * 2 + first, first % 2)
                body(k * 2 + (first + 1), (first + 1) % 2)
            for n in range(first + 2 * turns, hi):
                body(n, n % 2)

        def is_int(n):
            return isinstance(n, int)

        def has(n, low=0, high=n_img):
            return not is_int(n) or low <= n < high

        def cut(t, c, size=T):
            return t[:, c * size:(c + 1) * size]

        def low_hidden(eng, ops, n, b, c, j):
            g, s = n * NCH + c, sorted(SPLIT).index(j)
            eng.wait_ge(hh_ready, g * len(SPLIT) + s + 1)
            ops.tensor_tensor(hl[(b + c) % 2][:, s, :], hs[(b + c) % 2][:, j, :],
                              hh[(b + c) % 2][:, s, :].bitcast(f32), ALU.subtract).then_inc(hl_ready[SPLIT[j]], 1)

        MASK_STEPS = 7
        P1 = (1, n_img - 1)
        P2 = (1, n_img - 3)

        block = ctx.enter_context(nc.Block())

        @block.sync
        def _(sp):
            sp.dma_start(kt[:, :], consts).then_inc(params_in, 16)
            sp.dma_start(cw, cw_in.rearrange("o i h w -> o (i h w)")).then_inc(params_in, 16)
            for n in range(2):
                sp.dma_start(xb[n][:, :], x_v[n * C:(n + 1) * C, :]).then_inc(x_in_s[n], 16)
            for i, p in enumerate((cb_in, gamma_in, beta_in, b2_in)):
                sp.dma_start(cols[:, i:i + 1], p.rearrange("(c a) -> c a", a=1)).then_inc(params_in, 16)
            sp.dma_start(wr_c, wr_in).then_inc(params_in, 16)
            sp.dma_start(br_c, br_in.rearrange("(a n) -> a n", a=1).to_broadcast([C, 1])).then_inc(params_in, 16)
            for j in range(NB):
                sp.dma_start(b1c[:, j:j + 1], b1_in[j * C:(j + 1) * C].rearrange("(c a) -> c a", a=1)
                             ).then_inc(params_in, 16)
            sp.dma_start(w1_f, w1_in).then_inc(params_in, 16)
            sp.dma_start(w2_f[:, :, :], w2_in.rearrange("(n p) d -> p n d", p=C)).then_inc(params_in, 16)

            def phase1(n, b):
                if has(n + 2):
                    sp.wait_ge(split_ready, (n + 1) * NCH)
                    sp.dma_start(xb[b][:, :], x_v[bass.ds((n + 2) * C, C), :]).then_inc(x_in_s[b], 16)
                sp.wait_ge(y_copied, (n + 1) * NCH)
                sp.dma_start(y_dram[bass.ds(n * C, C), :], y16[b][:, :]).then_inc(y_saved[b], 16)

            pairs(sp, phase1, 1, n_img - 2, 0, n_img)

            def load(n, b):
                sp.dma_start(xb[b][:, :], x_v[bass.ds(n * C, C), :]).then_inc(xy_in[b], 16)
                sp.dma_start(y16[b][:, :], y_dram[bass.ds(n * C, C), :]).then_inc(xy_in[b], 16)

            for b in range(2):
                sp.wait_ge(y_saved[b], 16 * (n_img // 2))
            sp.wait_ge(bn_taken, n_img * NCH)
            load(0, 0)

            def phase2(n, b):
                if has(n):
                    sp.wait_ge(w_taken, n + 1)
                    sp.dma_start(w_dram[bass.ds(n, 1), :].rearrange("a (c t) -> (a c) t", t=T),
                                 wrow[:, :]).then_inc(w_saved, 16)
                    sp.wait_ge(w_saved, (n + 1) * 16)
                    w_n = w_dram[bass.ds(n, 1), :]
                    sp.dma_start(wse[:, :], w_n.rearrange("a (s t) -> s a t", s=SUB).to_broadcast([SUB, CAND, SLEN])
                                 ).then_inc(w_search_in, 16)
                    sp.dma_start(wk[:, :], w_n.rearrange("a (r t) -> (a r) t", t=MR_COLS)).then_inc(w_mask_in, 16)
                if has(n + 1):
                    sp.wait_ge(rms_ready, n + 2)
                    for q in range(2):
                        for s in range(2):
                            sp.dma_start(rows[32 * q + s:32 * q + s + 1, :].bitcast(f32)
                                         .rearrange("a (j p) -> a j p", p=TILE),
                                         rms[:, s, q, :].bitcast(f32)).then_inc(norm_rows_in, 16)
                if has(n - 1):
                    sp.wait_ge(out_ready, n * NCH)
                    sp.dma_start(out_v[bass.ds((n - 1) * C, C), :], yo[1 - b][:, :]).then_inc(out_saved[1 - b], 16)
                if has(n):
                    sp.wait_ge(gate_ready, n + 1)
                    for s in range(2):
                        sp.dma_start(rows[64 + s:65 + s, :].bitcast(f32)
                                     .rearrange("a (r t) -> a r t", t=MR_COLS),
                                     mks[:, s, :].bitcast(f32)).then_inc(gate_rows_in, 16)
                if has(n + 3):
                    if has(n + 1):
                        sp.wait_ge(base_ready, (n + 2) * NCH)
                    load(n + 3, 1 - b)

            pairs(sp, phase2, 1, n_img - 3, -2, n_img + 1)
            for b in range(2):
                sp.wait_ge(out_saved[b], 16 * (n_img // 2))

        @block.gpsimd
        def _(pool):
            nc.gpsimd.memset(wsel_h[:, :].bitcast(f32), 0.0).then_inc(prep_pool, 1)
            nc.gpsimd.memset(wsel_l[:, :].bitcast(f32), 0.0).then_inc(prep_pool, 1)
            pool.wait_ge(bound_ready, 1)
            nc.gpsimd.tensor_tensor(bound, bound2, half, ALU.pow).then_inc(bound_rooted, 1)
            pool.wait_ge(var_bn_ready, 1)
            nc.gpsimd.tensor_tensor(bn_r, bn_ve, kt[:, K_MHALF:K_MHALF + 1], ALU.pow).then_inc(bn_rooted, 1)

            def residual(n, b, c):
                pool.wait_ge(relu_ready, n * NCH + c + 1)
                nc.gpsimd.tensor_tensor(cut(xb[b], c), cut(xb[b], c), zr[(b + c) % 2][:, :],
                                        ALU.add).then_inc(x1_ready, 1)

            def low_part(n, b, c):
                pool.wait_ge(th_ready, n * NCH + c + 1)
                nc.gpsimd.tensor_tensor(cut(tl, c), tr[(b + c) % 2][:, :], cut(th, c).bitcast(f32),
                                        ALU.subtract).then_inc(tl_ready, 1)

            def phase2(n, b):
                for pos in range(POS + 1):
                    slot, j = divmod(pos, 2 * NB)
                    if pos < POS and SPLIT.get(j - 1) == "pool" and has(n):
                        low_hidden(pool, nc.gpsimd, n, b, slot, j - 1)
                    if pos == VAR_AT + 1 and has(n + 1):
                        pool.wait_ge(var_ready, n + 2)
                        nc.gpsimd.tensor_tensor(rm[:, 0, :], stw[:, 5, :], kt[0:TILE, K_MHALF:K_END],
                                                ALU.pow).then_inc(rstd_ready, 1)
                    if pos in RELU_AT and has(n + 2):
                        residual(n + 2, b, RELU_AT.index(pos))
                    if pos - 1 in NORM_AT and has(n + 1):
                        c = NORM_AT.index(pos - 1)
                        if has(n):
                            pool.wait_ge(h_done, (n * NCH + c + 1) * NB)
                        low_part(n + 1, 1 - b, c)

            pairs(pool, phase2, *P2, -2, n_img + 1)

        @block.scalar
        def _(act):
            act.wait_ge(cw_centred, 1)
            nc.scalar.activation(cwa, cwc, ACT.Abs, accum_out=abs_sum).then_inc(abs_summed, 1)
            nc.scalar.activation(cws, cwc.rearrange("o (i t) -> o t i", t=TAPS),
                                 ACT.Sign).then_inc(cw_signed, 1)
            for t in range(TAPS):
                act.wait_ge(cw_transposed, t + 1)
                nc.scalar.activation(cwT[:, t, :], ps[:, t % 2, 0:C // 2].bitcast(bf16),
                                     ACT.Copy).then_inc(cw_ready, 1)

            def sign(n, b, c):
                g = n * NCH + c
                act.wait_ge(centred, g + 1)
                if c == 0:
                    if has(n - 2):
                        act.wait_ge(conv_done, (n - 1) * NCH)
                    if is_int(n) and n == 0:
                        act.wait_ge(border_clear, 2)
                bank = CEN_BANK + (b + c) % 2
                nc.scalar.activation(sg[b][:, 1 + c * ROWS:1 + (c + 1) * ROWS, 1:1 + SIDE],
                                     ps[:, bank, 0:T].rearrange("p (r w) -> p r w", w=SIDE),
                                     ACT.Sign).then_inc(signed, 1)

            for c in range(NCH):
                sign(0, 0, c)

            def phase1(n, b):
                for c in range(NCH):
                    act.wait_ge(conv_done, n * NCH + c + 1)
                    if c == 0 and has(n - 2):
                        act.wait_ge(y_saved[b], (n - b) * 8)
                        act.wait_ge(bn_taken, (n - 1) * NCH)
                    nc.scalar.activation(cut(y16[b], c), ps[:, CONV_BANK + (b + c) % 2, 0:T],
                                         ACT.Copy).then_inc(y_copied, 1)
                    if has(n + 1):
                        sign(n + 1, 1 - b, c)

            pairs(act, phase1, 3, n_img - 1, 0, n_img)
            act.wait_ge(coef_ready, 2)

            def phase2(n, b):
                for pos in range(POS + 1):
                    slot, j = divmod(pos, 2 * NB)
                    if pos < POS and j < NB and has(n):
                        g = n * NCH + slot
                        act.wait_ge(h_done, g * NB + j + 1)
                        if j == 0:
                            wait_count(act, y_done, g - 1)
                        nc.scalar.activation(hs[(b + slot) % 2][:, j, :], ps[:, H_BANK + j, 0:T],
                                             ACT.Gelu_apprx_tanh, bias=b1c[:, j:j + 1]).then_inc(gelu_done, 1)
                        if j in SPLIT:
                            nc.scalar.activation(hh[(b + slot) % 2][:, sorted(SPLIT).index(j), :],
                                                 ps[:, H_BANK + j, 0:T], ACT.Gelu_apprx_tanh,
                                                 bias=b1c[:, j:j + 1]).then_inc(hh_ready, 1)
                    if j == 2 * NB - 1 and (has(n) and slot > 0 or slot == 0 and has(n - 1)):
                        c = (slot - 1) % NCH
                        m, mb = (n, b) if slot > 0 else (n - 1, 1 - b)
                        act.wait_ge(y_done, m * NCH + c + 1)
                        if c == 0 and has(m - 2):
                            act.wait_ge(out_saved[mb], (m - mb) * 8)
                        nc.scalar.activation(cut(yo[mb], c), ps[:, Y_BANK, 0:T], ACT.Identity,
                                             bias=b2_c).then_inc(y_taken, 1)
                    if pos in RELU_AT and has(n + 2):
                        c = RELU_AT.index(pos)
                        g = (n + 2) * NCH + c
                        if c == 0:
                            act.wait_ge(xy_in[b], (n + 2 - b) * 16 + 32)
                        wait_count(act, x1_ready, g - 1)
                        nc.scalar.activation(zr[(b + c) % 2][:, :], cut(y16[b], c), ACT.Relu,
                                             bias=bn_t[:, :], scale=bn_s[:, :]).then_inc(relu_ready, 1)
                    if pos - 1 in NORM_AT and has(n + 1):
                        c = NORM_AT.index(pos - 1)
                        if has(n):
                            act.wait_ge(h_done, (n * NCH + c + 1) * NB)
                        act.wait_ge(t_ready, (n + 1) * NCH + c + 1)
                        nc.scalar.activation(cut(th, c), tr[(1 - b + c) % 2][:, :],
                                             ACT.Copy).then_inc(th_ready, 1)

            pairs(act, phase2, 3, n_img - 3, -2, n_img + 1)

        @block.vector
        def _(dve):
            done = [0]

            def link(ins):
                done[0] += 1
                ins.then_inc(prep, 1)
                dve.wait_ge(prep, done[0])

            V = nc.vector
            for b in range(2):
                V.memset(sg[b], 0.0).then_inc(border_clear, 1)
            dve.wait_ge(params_in, 16 * N_PARAMS)
            V.tensor_copy(centre_r[:, :], kt[:, K_CEN:K_CEN + C]).then_inc(tables_ready, 1)

            def split(n, b, c):
                g = n * NCH + c
                if c == 0:
                    dve.wait_ge(x_in_s[b], (n - b) * 8 + 16)
                wait_count(dve, centred, g - 1)
                V.tensor_copy(xh[(b + c) % 2][:, :], cut(xb[b], c)).then_inc(xh_ready, 1)

            def split_low(n, b, c):
                dve.wait_ge(xh_ready, n * NCH + c + 1)
                V.tensor_tensor(xl[(b + c) % 2][:, :], cut(xb[b], c), xh[(b + c) % 2][:, :].bitcast(f32),
                                ALU.subtract).then_inc(split_ready, 1)

            link(V.tensor_reduce(wmean, cw.rearrange("o (i t) -> o t i", t=TAPS), AX.X, ALU.add))
            link(V.tensor_scalar(wmean, wmean, 1.0 / C, None, ALU.mult))
            cw3 = cw.rearrange("o (i t) -> o i t", t=TAPS)
            cwc3 = cwc.rearrange("o (i t) -> o i t", t=TAPS)
            for t in range(TAPS):
                last = V.tensor_scalar(cwc3[:, :, t], cw3[:, :, t], wmean[:, t:t + 1], -1.0, ALU.subtract, ALU.max)
            link(last)
            V.tensor_scalar(cwc, cwc, 1.0, None, ALU.min).then_inc(cw_centred, 1)
            V.tensor_copy(ident_b[:, :], ident).then_inc(tables_ready, 1)
            V.tensor_tensor(wr2, wr_c, wr_c, ALU.mult).then_inc(wr2_ready, 1)
            V.memset(half, 0.5)
            V.tensor_copy(same_b[:, :], kt[:, K_SAME:K_SAME + C])
            V.tensor_copy(flag_b[:, :], kt[:, K_FLAG:K_FLAG + C])
            V.tensor_copy(w1_h[:, :], w1_f)
            V.tensor_copy(w2_h[:, :, :], w2_f[:, :, :])
            V.tensor_copy(ones_r[:, :], kt[:, K_ONES:K_ONES + C])
            dve.wait_ge(prep_pool, 2)
            link(V.tensor_copy(wsel_h[:, C:C + 1], wr_c))
            V.tensor_tensor(w1_l[:, :], w1_f, w1_h[:, :].bitcast(f32), ALU.subtract)
            V.tensor_tensor(w2_l[:, :, :], w2_f[:, :, :], w2_h[:, :, :].bitcast(f32), ALU.subtract)
            link(V.tensor_tensor(wsel_l[:, C:C + 1], wr_c, wsel_h[:, C:C + 1].bitcast(f32), ALU.subtract))
            dve.wait_ge(wr2_summed, 1)
            V.tensor_scalar(bound2, ps[:, BC0, 0:1], float(C), 1e-30, ALU.mult, ALU.add).then_inc(bound_ready, 1)
            link(V.scalar_tensor_tensor(lo_c, br_c, -1.0, br_c, ALU.mult, ALU.max))
            dve.wait_ge(bound_rooted, 1)
            link(V.tensor_tensor(bound, bound, lo_c, ALU.add))
            link(V.tensor_scalar(bound.bitcast(i32), bound.bitcast(i32), 0x7F800000, None, ALU.bitwise_and))
            link(V.tensor_scalar(neg_b[:, :], bound, -2.0, None, ALU.mult))
            for r in range(ROUNDS):
                last = V.tensor_scalar(steps[:, r:r + 1], neg_b[:, :], -2.0 / CAND ** (r + 1), None, ALU.mult)
            link(last)
            link(V.tensor_scalar(candc[:, :], steps[:, :], kt[:, K_CIDX:K_CIDX + 1], None, ALU.mult))
            link(V.tensor_tensor(cand0[:, :], neg_b[:, :], candc[:, 0:1], ALU.add))

            for c in range(NCH):
                split(0, 0, c)
                split_low(0, 0, c)

            def batch_stats(n, b, c):
                g = n * NCH + c
                dve.wait_ge(y_copied, g + 1)
                V.bn_stats(bnst[:, bass.ds(g, 1), :], cut(y16[b], c)).then_inc(bn_taken, 1)

            def phase1(n, b):
                for c in range(NCH):
                    if has(n + 1):
                        split(n + 1, 1 - b, c)
                        split_low(n + 1, 1 - b, c)
                    if c:
                        batch_stats(n, b, c - 1)
                    elif has(n - 1):
                        batch_stats(n - 1, 1 - b, NCH - 1)

            pairs(dve, phase1, *P1, 0, n_img)

            batch_stats(n_img - 1, (n_img - 1) % 2, NCH - 1)

            dve.wait_ge(bn_taken, n_img * NCH)
            link(V.bn_aggr(bn_mv, bnst[:, :, :]))
            dve.wait_ge(abs_summed, 1)
            link(V.tensor_scalar(alpha[:, :], abs_sum, 1.0 / (C * TAPS), None, ALU.mult))
            link(V.scalar_tensor_tensor(mean_y, bn_mv[:, 0:1], alpha[:, :], cb_c, ALU.mult, ALU.add))
            link(V.tensor_scalar(bn_ve, bn_mv[:, 1:2], alpha[:, :], alpha[:, :], ALU.mult, ALU.mult))
            V.tensor_scalar(bn_ve, bn_ve, EPS, None, ALU.add).then_inc(var_bn_ready, 1)
            link(V.tensor_tensor(bias_d, cb_c, mean_y, ALU.subtract))
            dve.wait_ge(bn_rooted, 1)
            link(V.tensor_tensor(bn_r, bn_r, gamma_c, ALU.mult))
            V.tensor_tensor(bn_s[:, :], bn_r, alpha[:, :], ALU.mult).then_inc(coef_ready, 1)
            V.scalar_tensor_tensor(bn_t[:, :], bias_d, bn_r, beta_c, ALU.mult, ALU.add).then_inc(coef_ready, 1)

            def tile_stats(m, c):
                dve.wait_ge(transposed, m * NCH + c + 1)
                for i in range(TPG):
                    last = V.bn_stats(st[:, c * TPG + i, :], ps[0:TILE, T_BANK if c % 2 else BC0, i * C:(i + 1) * C])
                last.then_inc(stats_taken, 1)

            STAT_STEPS = 5
            mean2, dif, m2sum, sq, var_c, ve_c = (stw[:, i, :] for i in range(6))

            def link_stat(ins, m, j):
                ins.then_inc(stat_step, 1)
                dve.wait_ge(stat_step, m * STAT_STEPS + j)

            def token_variance(m):
                dve.wait_ge(stats_taken, (m + 1) * NCH)
                V.tensor_tensor(mean2, st[:, :, 1], st[:, :, 4], ALU.add)
                link_stat(V.tensor_tensor(dif, st[:, :, 1], st[:, :, 4], ALU.subtract), m, 1)
                V.tensor_tensor(m2sum, st[:, :, 2], st[:, :, 5], ALU.add)
                link_stat(V.tensor_tensor(sq, dif, dif, ALU.mult), m, 2)
                link_stat(V.scalar_tensor_tensor(var_c, sq, C / 4.0, m2sum, ALU.mult, ALU.add), m, 3)
                V.tensor_scalar(ve_c, var_c, 1.0 / C, EPS, ALU.mult, ALU.add).then_inc(var_ready, 1)

            def mean_over_std(m):
                dve.wait_ge(rstd_ready, m + 1)
                V.scalar_tensor_tensor(rm[:, 1, :], mean2, 0.5, rm[:, 0, :], ALU.mult, ALU.mult).then_inc(mr_ready, 1)

            def split_stats(m):
                dve.wait_ge(stat_rows, m + 1)
                src = ps[0:NT, T_BANK, 0:2 * C].rearrange("j (q p) -> j q p", q=2)[:, :, 0:TILE]
                link_stat(V.tensor_copy(rms[:, 0, :, :], src), m, 4)
                V.tensor_tensor(rms[:, 1, :, :], src, rms[:, 0, :, :].bitcast(f32),
                                ALU.subtract).then_inc(rms_ready, 1)
                V.tensor_copy(stw[0:1, 3, 0:1], stw[0:1, 2, 0:1]).then_inc(stat_step, 1)

            def scale_tokens(m, b, c):
                g = m * NCH + c
                ring = (b + c) % 2
                dve.wait_ge(bc_stats, 2 * g + 1)
                V.tensor_tensor(ur[ring][:, :], cut(xb[b], c), ps[:, BC0, 0:T], ALU.mult).then_inc(u_ready, 1)

            def centre_tokens(m, b, c):
                g = m * NCH + c
                ring = (b + c) % 2
                dve.wait_ge(bc_stats, 2 * g + 2)
                dve.wait_ge(u_ready, g + 1)
                wait_count(dve, th_ready, g - 1)
                wait_count(dve, tl_ready, g - 1)
                V.tensor_tensor(tr[ring][:, :], ur[ring][:, :], ps[:, BC1, 0:T], ALU.subtract).then_inc(t_ready, 1)

            def token_base(m, b, c):
                g = m * NCH + c
                ring = (b + c) % 2
                dve.wait_ge(t_ready, g + 1)
                V.tensor_tensor(cut(base[b], c), cut(xb[b], c), tr[ring][:, :], ALU.add).then_inc(base_ready, 1)

            def take_router(n):
                dve.wait_ge(w_done, n + 1)
                if has(n - 1):
                    dve.wait_ge(w_saved, n * 16)
                V.tensor_scalar(wrow[:, :], ps[0:NCH, T_BANK, 0:T], br_c[0:NCH, :], None,
                                ALU.add).then_inc(w_taken, 1)

            SEARCH_STEPS = 2 * ROUNDS - 1

            def count_above(n, r):
                if r == 0:
                    dve.wait_ge(w_search_in, (n + 1) * 16)
                else:
                    dve.wait_ge(search_step, n * SEARCH_STEPS + 2 * r)
                with nc.allow_low_precision(reason="integers up to SLEN"):
                    V.tensor_scalar(junk[:, :], wse[:, :], cand0[:, :] if r == 0 else cand_c, None, ALU.is_ge,
                                    ALU.add, accum_out=cnt_c).then_inc(search_dve, 1)

            def flag_candidates(n, r):
                dve.wait_ge(search_pe, n * 2 * ROUNDS + 2 * r + 1)
                V.tensor_scalar(flag_c, cnt_ps, float(TOP), None, ALU.is_ge).then_inc(search_dve, 1)

            def narrow(n, r):
                dve.wait_ge(search_pe, n * 2 * ROUNDS + 2 * r + 2)
                V.scalar_tensor_tensor(lo_c, idx_ps, steps[:, r:r + 1], neg_b[:, :] if r == 0 else lo_c,
                                       ALU.mult, ALU.add).then_inc(search_step, 1)
                dve.wait_ge(search_step, n * SEARCH_STEPS + 2 * r + 1)
                if r + 1 < ROUNDS:
                    V.tensor_tensor(cand_c, lo_c, candc[:, r + 1:r + 2], ALU.add).then_inc(search_step, 1)

            above, at_least, ties, keep, chosen, gate = (mk[:, i, :] for i in range(6))
            R = slice(0, MR_ROWS)

            def link_mask(ins, n, j):
                ins.then_inc(mask_step, 1)
                dve.wait_ge(mask_step, n * MASK_STEPS + j)

            def find_ties(n):
                dve.wait_ge(w_mask_in, (n + 1) * 16)
                V.tensor_scalar(at_least, wk[:, :], lo_c[R, :], 0.0, ALU.subtract, ALU.is_ge)
                link_mask(V.tensor_scalar(above, wk[:, :], lo_c[R, :], steps[R, ROUNDS - 1:ROUNDS],
                                          ALU.subtract, ALU.is_ge), n, 1)
                link_mask(V.tensor_tensor(ties, at_least, above, ALU.subtract), n, 2)
                V.tensor_reduce(rowg_c[R, :], above, AX.X, ALU.add)
                V.tensor_reduce(rowe_c[R, :], ties, AX.X, ALU.add).then_inc(ties_ready, 1)

            def copy_ties(n):
                dve.wait_ge(ties_t, n + 1)
                V.tensor_copy(et[:, :], ps[0:MR_COLS, T_BANK, 0:MR_ROWS])
                V.tensor_copy(off_c[R, :], off_ps).then_inc(ties_copied, 1)

            def gates(n):
                dve.wait_ge(ties_scanned, n + 1)
                dve.wait_ge(ties_copied, n + 1)
                link_mask(V.tensor_scalar(keep, ps[R, T_BANK, C:C + MR_COLS], off_c[R, :], float(TOP),
                                          ALU.add, ALU.is_le), n, 3)
                link_mask(V.tensor_tensor(keep, keep, ties, ALU.mult), n, 4)
                link_mask(V.tensor_tensor(chosen, above, keep, ALU.add), n, 5)
                link_mask(V.tensor_tensor(gate, chosen, wk[:, :], ALU.mult), n, 6)
                link_mask(V.tensor_copy(mks[:, 0, :], gate), n, 7)
                V.tensor_tensor(mks[:, 1, :], gate, mks[:, 0, :].bitcast(f32), ALU.subtract).then_inc(gate_ready, 1)

            def apply_gate(m, b, c):
                g = m * NCH + c
                dve.wait_ge(bc_gate, g + 1)
                dve.wait_ge(y_taken, g + 1)
                V.tensor_tensor(cut(yo[b], c), cut(yo[b], c), ps[:, BC1, 0:T], ALU.mult).then_inc(gated, 1)

            def add_base(m, b, c):
                g = m * NCH + c
                dve.wait_ge(gated, g + 1)
                dve.wait_ge(base_ready, g + 1)
                V.tensor_tensor(cut(yo[b], c), cut(yo[b], c), cut(base[b], c), ALU.add).then_inc(out_ready, 1)

            def phase2(n, b):
                for pos in range(POS):
                    slot, j = divmod(pos, 2 * NB)
                    if pos == WROW_AT + 1 and has(n):
                        take_router(n)
                    if pos in COUNT_AT and has(n):
                        flag_candidates(n, COUNT_AT.index(pos))
                    if pos in INDEX_AT and has(n):
                        r = INDEX_AT.index(pos)
                        narrow(n, r)
                        if r + 1 < ROUNDS:
                            count_above(n, r + 1)
                    if pos == COUNT_AT[0] - 1 and has(n):
                        count_above(n, 0)
                    if pos == INDEX_AT[-1] and has(n):
                        find_ties(n)
                    if pos == MASK_AT and has(n):
                        copy_ties(n)
                    if pos == SCAN_AT and has(n):
                        gates(n)
                    if SPLIT.get(j - 1) == "dve" and has(n):
                        low_hidden(dve, V, n, b, slot, j - 1)
                    if pos in TRANSPOSE_AT and has(n + 1):
                        tile_stats(n + 1, TRANSPOSE_AT.index(pos))
                    if pos == VAR_AT and has(n + 1):
                        token_variance(n + 1)
                    if pos == STAT_AT - 1 and has(n + 1):
                        mean_over_std(n + 1)
                    if pos == STAT_AT and has(n + 1):
                        split_stats(n + 1)
                    if pos in OUT_AT and has(n - 1):
                        apply_gate(n - 1, 1 - b, OUT_AT.index(pos))
                    if pos - 1 in OUT_AT and has(n - 1):
                        add_base(n - 1, 1 - b, OUT_AT.index(pos - 1))
                    if pos in NORM_AT and has(n + 1):
                        scale_tokens(n + 1, 1 - b, NORM_AT.index(pos))
                    if pos - 1 in NORM_AT and has(n + 1):
                        centre_tokens(n + 1, 1 - b, NORM_AT.index(pos - 1))
                    if pos - 2 in NORM_AT and has(n + 1):
                        token_base(n + 1, 1 - b, NORM_AT.index(pos - 2))

            pairs(dve, phase2, *P2, -1, n_img + 1)

        @block.tensor
        def _(pe):
            M = nc.tensor.matmul
            pe.wait_ge(wr2_ready, 1)
            M(ps[:, BC0, 0:1], kt[:, K_ONES:K_ONES + C], wr2, start=True, stop=True).then_inc(wr2_summed, 1)
            pe.wait_ge(tables_ready, 2)
            pe.wait_ge(cw_signed, 1)
            for t in range(TAPS):
                wait_count(pe, cw_ready, t - 1)
                nc.tensor.transpose(ps[:, t % 2, 0:C // 2].bitcast(bf16), cws[:, t, :],
                                    ident_b[:, :]).then_inc(cw_transposed, 1)
            pe.wait_ge(cw_ready, TAPS)

            def centre(n, b, c):
                g = n * NCH + c
                pe.wait_ge(split_ready, g + 1)
                wait_count(pe, signed, g - 1)
                bank = ps[:, CEN_BANK + (b + c) % 2, 0:T]
                M(bank, centre_r[:, :], xh[(b + c) % 2][:, :], start=True, stop=False)
                M(bank, centre_r[:, :], xl[(b + c) % 2][:, :], start=False, stop=True).then_inc(centred, 1)

            def conv(n, b, c):
                g = n * NCH + c
                pe.wait_ge(signed, n * NCH + min(c + 2, NCH))
                wait_count(pe, y_copied, g - 1)
                bank = ps[:, CONV_BANK + (b + c) % 2, 0:T].rearrange("p (r w) -> p r w", w=SIDE)
                for t in range(TAPS):
                    dy, dx = divmod(t, 3)
                    last = M(bank, cwT[:, t, :], sg[b][:, c * ROWS + dy:c * ROWS + dy + ROWS, dx:dx + SIDE],
                             start=t == 0, stop=t == TAPS - 1)
                last.then_inc(conv_done, 1)

            for c in range(NCH):
                centre(0, 0, c)

            def phase1(n, b):
                for c in range(NCH):
                    conv(n, b, c)
                    if has(n + 1):
                        centre(n + 1, 1 - b, c)

            pairs(pe, phase1, *P1, 0, n_img)
            pe.wait_ge(y_copied, n_img * NCH)
            pe.wait_ge(bn_taken, n_img * NCH)

            def transposes(m, b, c, n):
                pe.wait_ge(x1_ready, m * NCH + c + 1)
                if c == 0 and has(n):
                    pe.wait_ge(u_ready, (n + 1) * NCH)
                if c == 1 and has(n - 1):
                    pe.wait_ge(mask_step, (n - 1) * MASK_STEPS + 3)
                if c > 1:
                    pe.wait_ge(stats_taken, m * NCH + c - 1)
                if c > 1 and TRANSPOSE_AT[c - 2] < WROW_AT < TRANSPOSE_AT[c] and has(n):
                    pe.wait_ge(w_taken, n + 1)
                for i in range(TPG):
                    lo = c * T + i * TILE
                    last = nc.tensor.transpose(ps[0:TILE, T_BANK if c % 2 else BC0, i * C:(i + 1) * C], xb[b][:, lo:lo + TILE], ident)
                last.then_inc(transposed, 1)

            def router(n, b):
                pe.wait_ge(tl_ready, (n + 1) * NCH)
                if has(n + 1):
                    done = sum(p < WROW_AT for p in TRANSPOSE_AT)
                    pe.wait_ge(stats_taken, (n + 1) * NCH + done)
                elif has(n - 1):
                    pe.wait_ge(mask_step, (n - 1) * MASK_STEPS + 3)
                bank = ps[:, T_BANK, 0:T]
                for c in range(NCH):
                    for i, (w, t) in enumerate(((wsel_h, th), (wsel_h, tl), (wsel_l, th))):
                        last = M(bank, w[:, C - c:2 * C - c], cut(t, c), start=c == 0 and i == 0,
                                 stop=c == NCH - 1 and i == 2)
                last.then_inc(w_done, 1)

            def rows_of_stats(m, n):
                pe.wait_ge(mr_ready, m + 1)
                if has(n):
                    done = sum(p <= STAT_AT for p in COUNT_AT) + sum(p < STAT_AT for p in INDEX_AT)
                    pe.wait_ge(search_dve, n * 2 * ROUNDS + done + 1)
                for q in range(2):
                    last = nc.tensor.transpose(ps[0:NT, T_BANK, q * C:q * C + TILE], rm[:, q, :],
                                               ident[0:TILE, 0:TILE])
                last.then_inc(stat_rows, 1)

            def spread_stats(m, b, c, n, pos):
                g = m * NCH + c
                if c == 0:
                    pe.wait_ge(norm_rows_in, (m + 1) * 64)
                wait_count(pe, u_ready, g)
                M(ps[:, BC0, 0:T], ones_r[0:2, :], cut(rows[0:2, :], c), start=True, stop=True).then_inc(bc_stats, 1)
                wait_count(pe, t_ready, g)
                if has(n - 1):
                    pe.wait_ge(gated, (n - 1) * NCH + sum(p <= pos for p in OUT_AT))
                M(ps[:, BC1, 0:T], ones_r[32:34, :], cut(rows[32:34, :], c), start=True, stop=True).then_inc(bc_stats, 1)

            def spread_gates(m, b, c, n, pos):
                g = m * NCH + c
                if c == 0:
                    pe.wait_ge(gate_rows_in, (m + 1) * 32)
                if c:
                    pe.wait_ge(gated, g)
                if has(n + 1):
                    pe.wait_ge(t_ready, (n + 1) * NCH + sum(p < pos for p in NORM_AT))
                else:
                    pe.wait_ge(t_ready, (n if has(n) else n_img) * NCH + (NCH if has(n) else 0))
                M(ps[:, BC1, 0:T], ones_r[64:66, :], cut(rows[64:66, :], c), start=True, stop=True).then_inc(bc_gate, 1)

            def hidden(n, b, c, j):
                g = n * NCH + c
                if j == 0:
                    pe.wait_ge(tl_ready, g + 1)
                if j in SPLIT:
                    wait_count(pe, hh_ready, (g - 1) * len(SPLIT) + sorted(SPLIT).index(j) + 1)
                else:
                    wait_count(pe, gelu_done, (g - 1) * NB + j + 1)
                bank = ps[:, H_BANK + j, 0:T]
                blk = slice(j * C, (j + 1) * C)
                M(bank, w1_h[:, blk], cut(th, c), start=True, stop=False)
                M(bank, w1_h[:, blk], cut(tl, c), start=False, stop=False)
                M(bank, w1_l[:, blk], cut(th, c), start=False, stop=True).then_inc(h_done, 1)

            def output(n, b, c, j):
                g = n * NCH + c
                if j == 0:
                    wait_count(pe, y_taken, g)
                first, final = j == 0, j == NB - 1
                bank = ps[:, Y_BANK, 0:T]
                if j in SPLIT:
                    i = sorted(SPLIT).index(j)
                    same = [q for q in sorted(SPLIT) if SPLIT[q] == SPLIT[j]]
                    pe.wait_ge(hl_ready[SPLIT[j]], g * len(same) + same.index(j) + 1)
                    high, low = hh[(b + c) % 2][:, i, :], hl[(b + c) % 2][:, i, :]
                    pe.wait_ge(hh_ready, g * len(SPLIT) + i + 1)
                    M(bank, w2_h[:, j, :], high, start=first, stop=False)
                    M(bank, w2_h[:, j, :], low, start=False, stop=False)
                    last = M(bank, w2_l[:, j, :], high, start=False, stop=final)
                else:
                    pe.wait_ge(gelu_done, g * NB + j + 1)
                    last = M(bank, w2_f[:, j, :], hs[(b + c) % 2][:, j, :], start=first, stop=final)
                if j == NB - 1:
                    last.then_inc(y_done, 1)

            def count_candidates(n, r):
                pe.wait_ge(search_dve, n * 2 * ROUNDS + 2 * r + 1)
                if r == 0 and has(n + 1):
                    pe.wait_ge(stats_taken, (n + 2) * NCH)
                M(cnt_ps, same_b[:, :], cnt_c, start=True, stop=True).then_inc(search_pe, 1)

            def choose_candidate(n, r):
                pe.wait_ge(search_dve, n * 2 * ROUNDS + 2 * r + 2)
                if r == sum(p < STAT_AT for p in INDEX_AT) and has(n + 1):
                    pe.wait_ge(rms_ready, n + 2)
                M(idx_ps, flag_b[:, :], flag_c, start=True, stop=True).then_inc(search_pe, 1)

            def transpose_ties(n):
                pe.wait_ge(ties_ready, n + 1)
                R = slice(0, MR_ROWS)
                nc.tensor.transpose(ps[0:MR_COLS, T_BANK, 0:MR_ROWS], ties_sb, ident[R, R])
                M(off_ps, kt[R, K_ONES:K_ONES + MR_ROWS], rowg_c[R, :], start=True, stop=False)
                M(off_ps, kt[R, K_STRI:K_STRI + MR_ROWS], rowe_c[R, :], start=False, stop=True).then_inc(ties_t, 1)

            def scan_ties(n):
                pe.wait_ge(ties_copied, n + 1)
                M(ps[0:MR_ROWS, T_BANK, C:C + MR_COLS], et[:, :], kt[0:MR_COLS, K_TRIU:K_TRIU + MR_COLS],
                  start=True, stop=True).then_inc(ties_scanned, 1)

            def phase2(n, b):
                for pos in range(POS):
                    c, j = divmod(pos, 2 * NB)
                    if j < NB and has(n):
                        hidden(n, b, c, j)
                    if j >= NB and c > 0 and has(n):
                        output(n, b, c - 1, j - NB)
                    if j >= NB and c == 0 and has(n - 1):
                        output(n - 1, 1 - b, NCH - 1, j - NB)
                    if pos in TRANSPOSE_AT and has(n + 1):
                        transposes(n + 1, 1 - b, TRANSPOSE_AT.index(pos), n)
                    if pos == WROW_AT and has(n):
                        router(n, b)
                    if pos in COUNT_AT and has(n):
                        count_candidates(n, COUNT_AT.index(pos))
                    if pos in INDEX_AT and has(n):
                        choose_candidate(n, INDEX_AT.index(pos))
                    if pos == MASK_AT and has(n):
                        transpose_ties(n)
                    if pos == SCAN_AT and has(n):
                        scan_ties(n)
                    if pos == STAT_AT and has(n + 1):
                        rows_of_stats(n + 1, n)
                    if pos in OUT_AT and has(n - 1):
                        spread_gates(n - 1, 1 - b, OUT_AT.index(pos), n, pos)
                    if pos in NORM_AT and has(n + 1):
                        spread_stats(n + 1, 1 - b, NORM_AT.index(pos), n, pos)

            pairs(pe, phase2, *P2, -1, n_img + 1)


N_PARAMS = 14
_INS = ["x", "L0_conv_w", "L0_conv_b", "L0_conv_gamma", "L0_conv_beta", "L0_ffn_wr", "L0_ffn_br",
        "L0_ffn_w1", "L0_ffn_b1", "L0_ffn_w2", "L0_ffn_b2"]


def kernel(**inputs):
    import concourse.bacc as _bacc
    from concourse.bass_utils import run_bass_kernel_spmd as _run

    nc = _bacc.Bacc("TRN2", target_bir_lowering=False, num_devices=1)
    arrays = {"consts": constants()}
    for name in _INS:
        arrays[name] = np.ascontiguousarray(inputs[name])
    args = [nc.dram_tensor(name, a.shape, mybir.dt.from_np(a.dtype), kind="ExternalInput").ap()
            for name, a in arrays.items()]
    shape = arrays["x"].shape
    args.append(nc.dram_tensor("result", shape, mybir.dt.float32, kind="ExternalOutput").ap())
    block_kernel(nc, *args, shape[0])
    r = _run(nc, [arrays], core_ids=[0])
    return r.results[0]["result"]
```

```python
import numpy as np
import concourse.bass as bass
from concourse import mybir
from contextlib import ExitStack

C = 128
SIDE = 56
TOK = SIDE * SIDE
ROWS = 8
T = ROWS * SIDE
NCH = TOK // T
TAPS = 9
PAD = SIDE + 2
TILE = 112
NT = TOK // TILE
TPG = T // TILE
HID = 512
NB = HID // C
TOP = max(1, int(0.5 * TOK)) - 1
HALF = (NCH + 1) // 2
CAND = 16
SUB = C // CAND
SLEN = TOK // SUB
ROUNDS = 8
MR_ROWS, MR_COLS = 98, 32
EPS = 1e-5

K_ID, K_CEN, K_STRI, K_TRIU, K_ONES, K_CAND, K_CIDX, K_MHALF, K_END = (
    0, 128, 256, 384, 416, 544, 560, 561, 561 + NT)


def constants():
    t = np.zeros((C, K_END), np.float32)
    p, q = np.arange(C)[:, None], np.arange(C)[None, :]
    t[:, K_ID:K_ID + C] = p == q
    t[:, K_CEN:K_CEN + C] = (p == q) - 1.0 / C
    t[:, K_CAND:K_CAND + CAND - 1] = p % CAND == q[:, 1:CAND]
    t[:, K_STRI:K_STRI + C] = p < q
    t[:, K_TRIU:K_TRIU + MR_COLS] = p <= q[:, :MR_COLS]
    t[:, K_ONES:K_ONES + C] = 1.0
    t[:, K_CIDX] = np.arange(C) % CAND
    t[:, K_MHALF:K_END] = -0.5
    return t


POS = 2 * NB * NCH
RELU_AT = [9, 14, 18, 22, 37, 39, 45]
TRANSPOSE_AT = [1, 3, 4, 5, 9, 10, 11]
VAR_AT = 14
STAT_AT = 23
NORM_AT = [31, 39, 47, 54, 63, 71, 76]
BASE_AT = [34, 42, 52, 58, 65, 73, 79]
ROUTER_AT = [15, 16, 17, 20, 21, 23, 27]
COUNT_AT = [35, 39, 42, 46, 50, 53, 58, 61]
MASK_AT = 66
SCAN_AT = 69
OUT_AT = [19, 24, 29, 33, 38, 45, 52]
LOW_LAG = 4
POOL_LOW_BLOCKS = ((0, 1, 2, 3), (1,), (2,), (0, 1, 2, 3), (0, 1, 3), (0, 1, 2, 3), (0, 1, 2, 3))
POOL_LOW = [(c, j) for c, blocks in enumerate(POOL_LOW_BLOCKS) for j in blocks]


def block_kernel(nc, consts, x_in, cw_in, cb_in, gamma_in, beta_in, wr_in, br_in, w1_in, b1_in,
                 w2_in, b2_in, out, n_img):
    f32, f32r = mybir.dt.float32, mybir.dt.float32r
    bf16, f16, i32 = mybir.dt.bfloat16, mybir.dt.float16, mybir.dt.int32
    ALU = mybir.AluOpType
    ACT = mybir.ActivationFunctionType
    AX = mybir.AxisListType

    x_v = x_in.rearrange("b c h w -> (b c) (h w)")
    out_v = out.rearrange("b c h w -> (b c) (h w)")
    y_dram = nc.dram_tensor("y_int", [n_img * C, TOK], f16).ap()
    w_dram = nc.dram_tensor("w_row", [n_img, TOK], f32).ap()

    with ExitStack() as ctx:
        def sb(name, shape, dt):
            return ctx.enter_context(nc.sbuf_tensor(name, shape, dt))

        def sem(name):
            return ctx.enter_context(nc.semaphore(name))

        kt = sb("kt", [C, K_END], f32)
        ident = kt[:, K_ID:K_ID + C]
        centre_r = sb("centre_r", [C, C], f32r)
        ones_r = sb("ones_r", [C, C], f32r)
        cwT = sb("cwT", [C, TAPS, C], bf16)
        w1_h = sb("w1_h", [C, HID], f32r)
        w1_l = sb("w1_l", [C, HID], f32r)
        w2_h = sb("w2_h", [C, NB, C], f32r)
        w2_l = sb("w2_l", [C, NB, C], f32r)
        b1c = sb("b1c", [C, NB], f32)
        cols = sb("cols", [C, 8], f32)
        cb_c, gamma_c, beta_c, b2_c, wr_c, br_c = (cols[:, i:i + 1] for i in range(6))
        wsel_h = sb("wsel_h", [C, 2 * C], f32r)
        wsel_l = sb("wsel_l", [C, 2 * C], f32r)
        sm = sb("sm", [C, 32], f32)
        (wr2, bound2, bound, half, abs_sum, bn_ve, bn_r, mean_y, bias_d) = (sm[:, i:i + 1] for i in range(9))
        wmean = sm[:, 16:16 + TAPS]
        bn_mv = sm[:, 26:28]
        ident_b = sb("ident_b", [C, C], bf16)
        steps = sb("steps", [C, ROUNDS], f32)
        candc = sb("candc", [C, ROUNDS], f32)
        neg_b = sb("neg_b", [C, 1], f32)
        cand0 = sb("cand0", [C, 1], f32)
        alpha = sb("alpha", [C, 1], f32)
        bn_s = sb("bn_s", [C, 1], f32)
        bn_t = sb("bn_t", [C, 1], f32)

        xb = [sb(f"xb{b}", [C, TOK], f32) for b in range(2)]
        y16 = [sb(f"y16{b}", [C, TOK], f16) for b in range(2)]
        base = [sb(f"base{b}", [C, TOK], f32) for b in range(2)]
        yo = [sb(f"yo{b}", [C, TOK], f32) for b in range(2)]
        th = sb("th", [C, TOK], f32r)
        tl = sb("tl", [C, TOK], f32r)
        sg = [yo[b][:, 0:PAD * PAD // 2].bitcast(bf16).rearrange("p (r w) -> p r w", w=PAD) for b in range(2)]
        bnst = base[0][:, 0:n_img * NCH * 6].rearrange("p (g s) -> p g s", s=6)

        xh = [th[:, b * T:(b + 1) * T] for b in range(2)]
        xl = [tl[:, b * T:(b + 1) * T] for b in range(2)]
        zr = [sb(f"zr{b}", [C, T], f32) for b in range(2)]
        ur = [sb(f"ur{b}", [C, T], f32) for b in range(2)]
        tr = [sb(f"tr{b}", [C, T], f32) for b in range(2)]
        hs = sb("hs", [C, NB, T], f32)
        hh = [sb(f"hh{b}", [C, NB, T], f32r) for b in range(2)]
        hl = [sb(f"hl{b}", [C, NB, T], f32r) for b in range(2)]
        cw, cwc = (o[:, TOK - C * TAPS:TOK] for o in yo)
        cwa = base[1][:, 0:C * TAPS]
        cws = base[1][:, C * TAPS:C * TAPS * 3 // 2].bitcast(bf16).rearrange("o (t i) -> o t i", i=C)
        w1_f = base[1][:, 2 * C * TAPS:2 * C * TAPS + HID]
        w2_f = base[0][:, TOK - HID:TOK].rearrange("p (n d) -> p n d", d=C)
        rows = sb("rows", [C, TOK], f32r)
        st = sb("st", [TILE, NT, 6], f32)
        stw = sb("stw", [TILE, 6, NT], f32)
        rm = sb("rm", [TILE, 2, NT], f32)
        rms = sb("rms", [NT, 2, 2, TILE], f32r)
        wrow = sb("wrow", [NCH, T], f32)
        wse = sb("wse", [C, SLEN], f32)
        junk = sb("junk", [C, SLEN], bf16)
        wk = sb("wk", [MR_ROWS, MR_COLS], f32)
        mk = sb("mk", [MR_ROWS, 8, MR_COLS], f32)
        mks = sb("mks", [MR_ROWS, 2, MR_COLS], f32r)
        et = sb("et", [MR_COLS, MR_ROWS], f32)
        srch = sb("srch", [C, 8], f32)
        lo_c, cand_c, rowg_c, rowe_c, off_c, idx_c = (srch[:, i:i + 1] for i in range(6))
        cnt_c = sb("cnt_c", [C, 1], f16)
        cand_sel = sb("cand_sel", [C, CAND - 1], f16)
        reached = sb("reached", [C, CAND - 1], f32)

        ps = ctx.enter_context(nc.psum_tensor("ps", [C, 8, 512], f32))
        H_BANK, Y_BANK, T_BANK, BC0, BC1 = 0, 4, 5, 6, 7
        CEN_BANK, CONV_BANK = 0, 2
        ties_sb = mk[:, 2, :]
        cnt_ps = ps[:, T_BANK, 0:CAND - 1]
        off_ps = ps[0:MR_ROWS, T_BANK, T:T + 1]

        cw_loaded = sem("cw_loaded")
        kt_loaded = sem("kt_loaded")
        x0_begun = sem("x0_begun")
        params_in = sem("params_in")
        prep = sem("prep")
        prep_pool = sem("prep_pool")
        wr2_ready = sem("wr2_ready")
        wr2_summed = sem("wr2_summed")
        bound_ready = sem("bound_ready")
        bound_rooted = sem("bound_rooted")
        cw_centred = sem("cw_centred")
        abs_summed = sem("abs_summed")
        cw_signed = sem("cw_signed")
        cw_transposed = sem("cw_transposed")
        tables_ready = sem("tables_ready")
        var_bn_ready = sem("var_bn_ready")
        bn_rooted = sem("bn_rooted")
        cw_ready = sem("cw_ready")
        border_clear = sem("border_clear")
        x_in_s = [sem(f"x_in{b}") for b in range(2)]
        xh_ready = sem("xh_ready")
        split_ready = sem("split_ready")
        centred = sem("centred")
        signed = sem("signed")
        conv_done = sem("conv_done")
        y_copied = sem("y_copied")
        bn_taken = sem("bn_taken")
        y_saved = [sem(f"y_saved{b}") for b in range(2)]
        coef_ready = sem("coef_ready")
        xy_in = [[sem(f"xy_in{b}_{part}") for part in range(2)] for b in range(2)]
        relu_ready = sem("relu_ready")
        x1_ready = sem("x1_ready")
        transposed = sem("transposed")
        stats_taken = sem("stats_taken")
        stat_step = sem("stat_step")
        var_ready = sem("var_ready")
        rstd_ready = sem("rstd_ready")
        mr_ready = sem("mr_ready")
        stat_rows = sem("stat_rows")
        rms_h = sem("rms_h")
        rms_ready = sem("rms_ready")
        norm_rows_in = sem("norm_rows_in")
        bc_stats = sem("bc_stats")
        u_ready = sem("u_ready")
        t_ready = sem("t_ready")
        base_ready = sem("base_ready")
        th_ready = sem("th_ready")
        tl_ready = sem("tl_ready")
        w_done = sem("w_done")
        w_taken = sem("w_taken")
        w_saved = sem("w_saved")
        w_search_in = sem("w_search_in")
        w_mask_in = sem("w_mask_in")
        part_counts = sem("part_counts")
        counts_summed = sem("counts_summed")
        search_step = sem("search_step")
        mask_step = sem("mask_step")
        ties_ready = sem("ties_ready")
        ties_t = sem("ties_t")
        ties_copied = sem("ties_copied")
        ties_scanned = sem("ties_scanned")
        gate_ready = sem("gate_ready")
        gate_rows_in = sem("gate_rows_in")
        bc_gate = sem("bc_gate")
        h_done = sem("h_done")
        hh_ready = sem("hh_ready")
        hl_dve = sem("hl_dve")
        hl_pool = sem("hl_pool")
        y_done = sem("y_done")
        y_taken = sem("y_taken")
        gated = sem("gated")
        out_ready = sem("out_ready")
        out_saved = [sem(f"out_saved{b}") for b in range(2)]

        def wait_count(eng, semaphore, value):
            if not (isinstance(value, int) and value <= 0):
                eng.wait_ge(semaphore, value)

        def pairs(eng, body, first, last, lo, hi):
            for n in range(lo, first):
                body(n, n % 2)
            turns = (last - first) // 2
            with eng.Fori(0, turns) as k:
                body(k * 2 + first, first % 2)
                body(k * 2 + (first + 1), (first + 1) % 2)
            for n in range(first + 2 * turns, hi):
                body(n, n % 2)

        def is_int(n):
            return isinstance(n, int)

        def has(n, low=0, high=n_img):
            return not is_int(n) or low <= n < high

        def cut(t, c, size=T):
            return t[:, c * size:(c + 1) * size]

        LOW_PART_AT = [p + 1 for p in NORM_AT]

        def due(table, shift, n, b, pos):
            steps = [table] if is_int(table) else table
            found = []
            for at, m, mb in ((pos, n + shift, (b + shift) % 2), (pos + POS, n + shift - 1, (b + shift + 1) % 2)):
                if at in steps and has(m):
                    found.append((m, mb, steps.index(at)))
            return found

        def done(table, shift, n, pos):
            steps = [table] if is_int(table) else table
            if is_int(n):
                return sum((m - shift) * POS + p < n * POS + pos for m in range(n_img) for p in steps)
            return (n + shift) * len(steps) + (sum(p < pos for p in steps) - sum(p - POS >= pos for p in steps))

        low_blocks = {True: sorted(POOL_LOW),
                      False: sorted({(c, j) for c in range(NCH) for j in range(NB)} - set(POOL_LOW))}

        def wait_low(eng, n, c, j):
            on_pool = (c, j) in POOL_LOW
            rank, total = low_blocks[on_pool].index((c, j)), len(low_blocks[on_pool])
            eng.wait_ge(hl_pool if on_pool else hl_dve, n * total + rank + 1)

        def low_hidden(eng, ops, n, b, pos, on_pool):
            c, j = divmod(pos - LOW_LAG, 2 * NB)
            if j < NB and c >= 0 and ((c, j) in POOL_LOW) == on_pool and has(n):
                eng.wait_ge(hh_ready, (n * NCH + c) * NB + j + 1)
                ops.tensor_tensor(hl[(b + c) % 2][:, j, :], hs[:, j, :], hh[(b + c) % 2][:, j, :].bitcast(f32),
                                  ALU.subtract).then_inc(hl_pool if on_pool else hl_dve, 1)

        MASK_STEPS = 7
        PART = (slice(0, HALF * T), slice(HALF * T, TOK))
        P1 = (1, n_img - 1)
        P2 = (3, n_img - 3)

        block = ctx.enter_context(nc.Block())

        @block.sync
        def _(sp):
            sp.dma_start(cw, cw_in.rearrange("o i h w -> o (i h w)")).then_inc(cw_loaded, 16)
            sp.dma_start(xb[0][:, 0:HALF * T], x_v[0:C, 0:HALF * T]).then_inc(x0_begun, 16)
            sp.dma_start(xb[0][:, HALF * T:TOK], x_v[0:C, HALF * T:TOK]).then_inc(x_in_s[0], 16)
            sp.dma_start(xb[1][:, :], x_v[C:2 * C, :]).then_inc(x_in_s[1], 16)
            sp.dma_start(w1_f, w1_in).then_inc(params_in, 16)
            sp.dma_start(w2_f, w2_in.rearrange("(n p) d -> p n d", p=C)).then_inc(params_in, 16)
            for i, p in enumerate((cb_in, gamma_in, beta_in, b2_in)):
                sp.dma_start(cols[:, i:i + 1], p.rearrange("(c a) -> c a", a=1)).then_inc(params_in, 16)
            sp.dma_start(wr_c, wr_in).then_inc(params_in, 16)
            sp.dma_start(br_c, br_in.rearrange("(a n) -> a n", a=1).to_broadcast([C, 1])).then_inc(params_in, 16)
            for j in range(NB):
                sp.dma_start(b1c[:, j:j + 1], b1_in[j * C:(j + 1) * C].rearrange("(c a) -> c a", a=1)
                             ).then_inc(params_in, 16)

            def load_x(n, b, part):
                sp.dma_start(xb[b][:, PART[part]], x_v[bass.ds(n * C, C), PART[part]]).then_inc(xy_in[b][part], 16)

            def load_y(n, b, part):
                sp.dma_start(y16[b][:, PART[part]], y_dram[bass.ds(n * C, C), PART[part]]
                             ).then_inc(xy_in[b][part], 16)

            def phase1(n, b):
                sp.wait_ge(split_ready, (n + 1) * NCH)
                if has(n + 2):
                    sp.dma_start(xb[b][:, :], x_v[bass.ds((n + 2) * C, C), :]).then_inc(x_in_s[b], 16)
                else:
                    for part in range(2):
                        load_x(n + 2 - n_img, b, part)
                sp.wait_ge(y_copied, (n + 1) * NCH)
                sp.dma_start(y_dram[bass.ds(n * C, C), :], y16[b][:, :]).then_inc(y_saved[b], 16)

            pairs(sp, phase1, 1, n_img - 2, 0, n_img)
            for b in range(2):
                sp.wait_ge(y_saved[b], 16 * (n_img // 2))
                sp.wait_ge(bn_taken, (n_img - 1 + b) * NCH)
                for part in range(2):
                    load_y(b, b, part)

            def store(n, b, part):
                sp.wait_ge(out_ready, n * NCH + (HALF, NCH)[part])
                sp.dma_start(out_v[bass.ds(n * C, C), PART[part]], yo[b][:, PART[part]]).then_inc(out_saved[b], 16)

            def phase2(n, b):
                if has(n + 2, 2):
                    sp.wait_ge(base_ready, n * NCH + HALF)
                    load_x(n + 2, b, 0)
                    load_y(n + 2, b, 0)
                if has(n - 1):
                    sp.wait_ge(gate_ready, n)
                    for s in range(2):
                        sp.dma_start(rows[64 + s:65 + s, :].bitcast(f32)
                                     .rearrange("a (r t) -> a r t", t=MR_COLS),
                                     mks[:, s, :].bitcast(f32)).then_inc(gate_rows_in, 16)
                if has(n + 1):
                    sp.wait_ge(rms_ready, n + 2)
                    for q in range(2):
                        for s in range(2):
                            sp.dma_start(rows[32 * q + s:32 * q + s + 1, :].bitcast(f32)
                                         .rearrange("a (j p) -> a j p", p=TILE),
                                         rms[:, s, q, :].bitcast(f32)).then_inc(norm_rows_in, 16)
                if has(n):
                    sp.wait_ge(w_taken, n + 1)
                    sp.dma_start(w_dram[bass.ds(n, 1), :].rearrange("a (c t) -> (a c) t", t=T),
                                 wrow[:, :]).then_inc(w_saved, 16)
                    sp.wait_ge(w_saved, (n + 1) * 16)
                    w_n = w_dram[bass.ds(n, 1), :]
                    sp.dma_start(wse[:, :], w_n.rearrange("a (s t) -> s a t", s=SUB).to_broadcast([SUB, CAND, SLEN])
                                 ).then_inc(w_search_in, 16)
                    sp.dma_start(wk[:, :], w_n.rearrange("a (r t) -> (a r) t", t=MR_COLS)).then_inc(w_mask_in, 16)
                if has(n + 2, 2):
                    sp.wait_ge(base_ready, (n + 1) * NCH)
                    load_x(n + 2, b, 1)
                    load_y(n + 2, b, 1)
                if has(n - 1):
                    store(n - 1, 1 - b, 0)
                    store(n - 1, 1 - b, 1)

            pairs(sp, phase2, *P2, -2, n_img + 1)
            for b in range(2):
                sp.wait_ge(out_saved[b], 32 * (n_img // 2))

        @block.gpsimd
        def _(pool):
            for b in range(2):
                nc.gpsimd.memset(sg[b], 0.0).then_inc(border_clear, 1)
            nc.gpsimd.memset(wsel_h[:, :].bitcast(f32), 0.0).then_inc(prep_pool, 1)
            nc.gpsimd.memset(wsel_l[:, :].bitcast(f32), 0.0).then_inc(prep_pool, 1)
            pool.wait_ge(var_bn_ready, 1)
            nc.gpsimd.tensor_tensor(bn_r, bn_ve, kt[:, K_MHALF:K_MHALF + 1], ALU.pow).then_inc(bn_rooted, 1)
            pool.wait_ge(bound_ready, 1)
            nc.gpsimd.tensor_tensor(bound, bound2, half, ALU.pow).then_inc(bound_rooted, 1)

            def residual(n, b, c):
                pool.wait_ge(relu_ready, n * NCH + c + 1)
                nc.gpsimd.tensor_tensor(cut(xb[b], c), cut(xb[b], c), zr[(b + c) % 2][:, :],
                                        ALU.add).then_inc(x1_ready, 1)

            def low_part(n, b, c):
                pool.wait_ge(th_ready, n * NCH + c + 1)
                nc.gpsimd.tensor_tensor(cut(tl, c), tr[(b + c) % 2][:, :], cut(th, c).bitcast(f32),
                                        ALU.subtract).then_inc(tl_ready, 1)

            def phase2(n, b):
                for pos in range(POS):
                    low_hidden(pool, nc.gpsimd, n, b, pos, True)
                    for m, mb, _ in due(VAR_AT + 1, 1, n, b, pos):
                        pool.wait_ge(var_ready, m + 1)
                        nc.gpsimd.tensor_tensor(rm[:, 0, :], stw[:, 5, :], kt[0:TILE, K_MHALF:K_END],
                                                ALU.pow).then_inc(rstd_ready, 1)
                    for m, mb, c in due(RELU_AT, 2, n, b, pos):
                        residual(m, mb, c)
                    for m, mb, c in due(LOW_PART_AT, 1, n, b, pos):
                        if has(m - 1):
                            pool.wait_ge(h_done, ((m - 1) * NCH + c + 1) * NB)
                            pool.wait_ge(w_done, m)
                        low_part(m, mb, c)

            pairs(pool, phase2, *P2, -2, n_img + 1)

        @block.scalar
        def _(act):
            act.dma_start(kt[:, :], consts).then_inc(kt_loaded, 16)
            act.wait_ge(cw_centred, 1)
            nc.scalar.activation(cwa, cwc, ACT.Abs, accum_out=abs_sum).then_inc(abs_summed, 1)
            nc.scalar.activation(cws, cwc.rearrange("o (i t) -> o t i", t=TAPS),
                                 ACT.Sign).then_inc(cw_signed, 1)
            for t in range(TAPS):
                act.wait_ge(cw_transposed, t + 1)
                nc.scalar.activation(cwT[:, t, :], ps[:, t % 2, 0:C // 2].bitcast(bf16),
                                     ACT.Copy).then_inc(cw_ready, 1)

            def sign(n, b, c):
                g = n * NCH + c
                act.wait_ge(centred, g + 1)
                if c == 0:
                    if has(n - 2):
                        act.wait_ge(conv_done, (n - 1) * NCH)
                    if is_int(n) and n < 2:
                        act.wait_ge(border_clear, n + 1)
                bank = CEN_BANK + (b + c) % 2
                nc.scalar.activation(sg[b][:, 1 + c * ROWS:1 + (c + 1) * ROWS, 1:1 + SIDE],
                                     ps[:, bank, 0:T].rearrange("p (r w) -> p r w", w=SIDE),
                                     ACT.Sign).then_inc(signed, 1)

            for c in range(NCH):
                sign(0, 0, c)

            def phase1(n, b):
                for c in range(NCH):
                    act.wait_ge(conv_done, n * NCH + c + 1)
                    if c == 0 and has(n - 2):
                        act.wait_ge(y_saved[b], (n - b) * 8)
                        act.wait_ge(bn_taken, (n - 1) * NCH)
                    nc.scalar.activation(cut(y16[b], c), ps[:, CONV_BANK + (b + c) % 2, 0:T],
                                         ACT.Copy).then_inc(y_copied, 1)
                    if has(n + 1):
                        sign(n + 1, 1 - b, c)

            pairs(act, phase1, 3, n_img - 1, 0, n_img)
            act.wait_ge(coef_ready, 2)

            def phase2(n, b):
                for pos in range(POS):
                    slot, j = divmod(pos, 2 * NB)
                    if j < NB and has(n):
                        g = n * NCH + slot
                        act.wait_ge(h_done, g * NB + j + 1)
                        if j == 0:
                            wait_count(act, y_done, g - 1)
                        if slot > 0:
                            wait_low(act, n, slot - 1, j)
                        elif has(n - 1):
                            wait_low(act, n - 1, NCH - 1, j)
                        nc.scalar.activation(hs[:, j, :], ps[:, H_BANK + j, 0:T],
                                             ACT.Gelu_apprx_tanh, bias=b1c[:, j:j + 1])
                        nc.scalar.activation(hh[(b + slot) % 2][:, j, :], ps[:, H_BANK + j, 0:T],
                                             ACT.Gelu_apprx_tanh, bias=b1c[:, j:j + 1]).then_inc(hh_ready, 1)
                    if j == 2 * NB - 1 and (has(n) and slot > 0 or slot == 0 and has(n - 1)):
                        c = (slot - 1) % NCH
                        m, mb = (n, b) if slot > 0 else (n - 1, 1 - b)
                        act.wait_ge(y_done, m * NCH + c + 1)
                        if c == 0 and has(m - 2):
                            act.wait_ge(out_saved[mb], (m - mb) * 16)
                        nc.scalar.activation(cut(yo[mb], c), ps[:, Y_BANK, 0:T], ACT.Identity,
                                             bias=b2_c).then_inc(y_taken, 1)
                    for m, mb, c in due(RELU_AT, 2, n, b, pos):
                        if c in (0, HALF):
                            act.wait_ge(xy_in[mb][c // HALF], (m - mb) * 16 + 32)
                        wait_count(act, x1_ready, m * NCH + c - 1)
                        nc.scalar.activation(zr[(mb + c) % 2][:, :], cut(y16[mb], c), ACT.Relu,
                                             bias=bn_t[:, :], scale=bn_s[:, :]).then_inc(relu_ready, 1)
                    for m, mb, c in due(LOW_PART_AT, 1, n, b, pos):
                        if has(m - 1):
                            act.wait_ge(h_done, ((m - 1) * NCH + c + 1) * NB)
                            act.wait_ge(w_done, m)
                        act.wait_ge(t_ready, m * NCH + c + 1)
                        nc.scalar.activation(cut(th, c), tr[(mb + c) % 2][:, :], ACT.Copy).then_inc(th_ready, 1)

            pairs(act, phase2, *P2, -2, n_img + 1)

        @block.vector
        def _(dve):
            done = [0]

            def link(ins):
                done[0] += 1
                ins.then_inc(prep, 1)
                dve.wait_ge(prep, done[0])

            V = nc.vector
            dve.wait_ge(kt_loaded, 16)
            V.tensor_copy(ident_b[:, :], ident).then_inc(tables_ready, 1)
            V.tensor_copy(centre_r[:, :], kt[:, K_CEN:K_CEN + C]).then_inc(tables_ready, 1)

            def split(n, b, c):
                g = n * NCH + c
                if is_int(n) and n == 0:
                    if c in (0, HALF):
                        dve.wait_ge(x_in_s[0] if c else x0_begun, 16)
                elif c == 0:
                    dve.wait_ge(x_in_s[b], (n - b) * 8 + 16)
                wait_count(dve, centred, g - 1)
                V.tensor_copy(xh[(b + c) % 2][:, :], cut(xb[b], c)).then_inc(xh_ready, 1)

            def split_low(n, b, c):
                dve.wait_ge(xh_ready, n * NCH + c + 1)
                V.tensor_tensor(xl[(b + c) % 2][:, :], cut(xb[b], c), xh[(b + c) % 2][:, :].bitcast(f32),
                                ALU.subtract).then_inc(split_ready, 1)

            dve.wait_ge(cw_loaded, 16)
            link(V.tensor_reduce(wmean, cw.rearrange("o (i t) -> o t i", t=TAPS), AX.X, ALU.add))
            link(V.tensor_scalar(wmean, wmean, 1.0 / C, None, ALU.mult))
            cw3 = cw.rearrange("o (i t) -> o i t", t=TAPS)
            cwc3 = cwc.rearrange("o (i t) -> o i t", t=TAPS)
            for t in range(TAPS):
                last = V.tensor_scalar(cwc3[:, :, t], cw3[:, :, t], wmean[:, t:t + 1], -1.0, ALU.subtract, ALU.max)
            link(last)
            V.tensor_scalar(cwc, cwc, 1.0, None, ALU.min).then_inc(cw_centred, 1)
            for c in range(NCH):
                split(0, 0, c)
                split_low(0, 0, c)

            def batch_stats(n, b, c):
                g = n * NCH + c
                dve.wait_ge(y_copied, g + 1)
                V.bn_stats(bnst[:, bass.ds(g, 1), :], cut(y16[b], c)).then_inc(bn_taken, 1)

            def phase1(n, b):
                for c in range(NCH):
                    if has(n + 1):
                        split(n + 1, 1 - b, c)
                        split_low(n + 1, 1 - b, c)
                    if c:
                        batch_stats(n, b, c - 1)
                    elif has(n - 1):
                        batch_stats(n - 1, 1 - b, NCH - 1)

            phase1(0, 0)
            dve.wait_ge(params_in, 16 * N_PARAMS)
            V.tensor_tensor(wr2, wr_c, wr_c, ALU.mult).then_inc(wr2_ready, 1)
            V.memset(half, 0.5)
            V.tensor_copy(cand_sel[:, :], kt[:, K_CAND:K_CAND + CAND - 1])
            V.tensor_copy(w1_h[:, :], w1_f)
            V.tensor_copy(w2_h[:, :, :], w2_f)
            V.tensor_copy(ones_r[:, :], kt[:, K_ONES:K_ONES + C])
            dve.wait_ge(prep_pool, 2)
            link(V.tensor_copy(wsel_h[:, C:C + 1], wr_c))
            V.tensor_tensor(w1_l[:, :], w1_f, w1_h[:, :].bitcast(f32), ALU.subtract)
            V.tensor_tensor(w2_l[:, :, :], w2_f, w2_h[:, :, :].bitcast(f32), ALU.subtract)
            link(V.tensor_tensor(wsel_l[:, C:C + 1], wr_c, wsel_h[:, C:C + 1].bitcast(f32), ALU.subtract))

            pairs(dve, phase1, *P1, 1, n_img)

            batch_stats(n_img - 1, (n_img - 1) % 2, NCH - 1)

            dve.wait_ge(bn_taken, n_img * NCH)
            link(V.bn_aggr(bn_mv, bnst[:, :, :]))
            dve.wait_ge(abs_summed, 1)
            link(V.tensor_scalar(alpha[:, :], abs_sum, 1.0 / (C * TAPS), None, ALU.mult))
            link(V.scalar_tensor_tensor(mean_y, bn_mv[:, 0:1], alpha[:, :], cb_c, ALU.mult, ALU.add))
            link(V.tensor_scalar(bn_ve, bn_mv[:, 1:2], alpha[:, :], alpha[:, :], ALU.mult, ALU.mult))
            V.tensor_scalar(bn_ve, bn_ve, EPS, None, ALU.add).then_inc(var_bn_ready, 1)
            link(V.tensor_tensor(bias_d, cb_c, mean_y, ALU.subtract))
            dve.wait_ge(bn_rooted, 1)
            link(V.tensor_tensor(bn_r, bn_r, gamma_c, ALU.mult))
            V.tensor_tensor(bn_s[:, :], bn_r, alpha[:, :], ALU.mult).then_inc(coef_ready, 1)
            V.scalar_tensor_tensor(bn_t[:, :], bias_d, bn_r, beta_c, ALU.mult, ALU.add).then_inc(coef_ready, 1)

            dve.wait_ge(wr2_summed, 1)
            V.tensor_scalar(bound2, ps[:, BC0, 0:1], float(C), 1e-30, ALU.mult, ALU.add).then_inc(bound_ready, 1)
            link(V.scalar_tensor_tensor(lo_c, br_c, -1.0, br_c, ALU.mult, ALU.max))
            dve.wait_ge(bound_rooted, 1)
            link(V.tensor_tensor(bound, bound, lo_c, ALU.add))
            link(V.tensor_scalar(bound.bitcast(i32), bound.bitcast(i32), 0x7F800000, None, ALU.bitwise_and))
            link(V.tensor_scalar(neg_b[:, :], bound, -2.0, None, ALU.mult))
            for r in range(ROUNDS):
                last = V.tensor_scalar(steps[:, r:r + 1], neg_b[:, :], -2.0 / CAND ** (r + 1), None, ALU.mult)
            link(last)
            link(V.tensor_scalar(candc[:, :], steps[:, :], kt[:, K_CIDX:K_CIDX + 1], None, ALU.mult))
            link(V.tensor_tensor(cand0[:, :], neg_b[:, :], candc[:, 0:1], ALU.add))

            def tile_stats(m, c):
                dve.wait_ge(transposed, m * NCH + c + 1)
                for i in range(TPG):
                    last = V.bn_stats(st[:, c * TPG + i, :], ps[0:TILE, BC0 + c % 2, i * C:(i + 1) * C])
                last.then_inc(stats_taken, 1)

            STAT_STEPS = 4
            mean2, dif, m2sum, sq, var_c, ve_c = (stw[:, i, :] for i in range(6))

            def link_stat(ins, m, j):
                ins.then_inc(stat_step, 1)
                dve.wait_ge(stat_step, m * STAT_STEPS + j)

            def token_variance(m):
                dve.wait_ge(stats_taken, (m + 1) * NCH)
                V.tensor_tensor(mean2, st[:, :, 1], st[:, :, 4], ALU.add)
                link_stat(V.tensor_tensor(dif, st[:, :, 1], st[:, :, 4], ALU.subtract), m, 1)
                V.tensor_tensor(m2sum, st[:, :, 2], st[:, :, 5], ALU.add)
                link_stat(V.tensor_tensor(sq, dif, dif, ALU.mult), m, 2)
                link_stat(V.scalar_tensor_tensor(var_c, sq, C / 4.0, m2sum, ALU.mult, ALU.add), m, 3)
                V.tensor_scalar(ve_c, var_c, 1.0 / C, EPS, ALU.mult, ALU.add).then_inc(var_ready, 1)

            def mean_over_std(m):
                dve.wait_ge(rstd_ready, m + 1)
                V.scalar_tensor_tensor(rm[:, 1, :], mean2, 0.5, rm[:, 0, :], ALU.mult, ALU.mult).then_inc(mr_ready, 1)

            def split_stats(m):
                dve.wait_ge(stat_rows, m + 1)
                src = ps[0:NT, BC0, 0:2 * C].rearrange("j (q p) -> j q p", q=2)[:, :, 0:TILE]
                link_stat(V.tensor_copy(rms[:, 0, :, :], src), m, 4)
                V.tensor_tensor(rms[:, 1, :, :], src, rms[:, 0, :, :].bitcast(f32),
                                ALU.subtract).then_inc(rms_ready, 1)

            def scale_tokens(m, b, c):
                g = m * NCH + c
                ring = (b + c) % 2
                dve.wait_ge(bc_stats, 2 * g + 1)
                V.tensor_tensor(ur[ring][:, :], cut(xb[b], c), ps[:, BC0, 0:T], ALU.mult).then_inc(u_ready, 1)

            def centre_tokens(m, b, c):
                g = m * NCH + c
                ring = (b + c) % 2
                dve.wait_ge(bc_stats, 2 * g + 2)
                dve.wait_ge(u_ready, g + 1)
                wait_count(dve, th_ready, g - 1)
                wait_count(dve, tl_ready, g - 1)
                V.tensor_tensor(tr[ring][:, :], ur[ring][:, :], ps[:, BC1, 0:T], ALU.subtract).then_inc(t_ready, 1)

            def token_base(m, b, c):
                g = m * NCH + c
                ring = (b + c) % 2
                dve.wait_ge(t_ready, g + 1)
                V.tensor_tensor(cut(base[b], c), cut(xb[b], c), tr[ring][:, :], ALU.add).then_inc(base_ready, 1)

            def take_router(n):
                dve.wait_ge(w_done, n + 1)
                if has(n - 1):
                    dve.wait_ge(w_saved, n * 16)
                V.tensor_scalar(wrow[:, :], ps[0:NCH, T_BANK, 0:T], br_c[0:NCH, :], None,
                                ALU.add).then_inc(w_taken, 1)

            SEARCH_STEPS = 3 * ROUNDS - 1

            def count_above(n, r):
                if r == 0:
                    dve.wait_ge(w_search_in, (n + 1) * 16)
                else:
                    dve.wait_ge(search_step, n * SEARCH_STEPS + 3 * r)
                with nc.allow_low_precision(reason="integers up to SLEN"):
                    V.tensor_scalar(junk[:, :], wse[:, :], cand0[:, :] if r == 0 else cand_c, None, ALU.is_ge,
                                    ALU.add, accum_out=cnt_c[:, :]).then_inc(part_counts, 1)

            def choose(n, r):
                dve.wait_ge(counts_summed, n * ROUNDS + r + 1)
                V.tensor_scalar(reached[:, :], cnt_ps, float(TOP), None, ALU.is_ge, ALU.add,
                                accum_out=idx_c).then_inc(search_step, 1)

            def raise_end(n, r):
                dve.wait_ge(search_step, n * SEARCH_STEPS + 3 * r + 1)
                V.scalar_tensor_tensor(lo_c, idx_c, steps[:, r:r + 1], neg_b[:, :] if r == 0 else lo_c,
                                       ALU.mult, ALU.add).then_inc(search_step, 1)

            def next_candidate(n, r):
                dve.wait_ge(search_step, n * SEARCH_STEPS + 3 * r + 2)
                if r + 1 < ROUNDS:
                    V.tensor_tensor(cand_c, lo_c, candc[:, r + 1:r + 2], ALU.add).then_inc(search_step, 1)

            above, at_least, ties, keep, chosen, gate = (mk[:, i, :] for i in range(6))
            R = slice(0, MR_ROWS)

            def link_mask(ins, n, j):
                ins.then_inc(mask_step, 1)
                dve.wait_ge(mask_step, n * MASK_STEPS + j)

            def find_ties(n):
                dve.wait_ge(w_mask_in, (n + 1) * 16)
                V.tensor_scalar(at_least, wk[:, :], lo_c[R, :], 0.0, ALU.subtract, ALU.is_ge)
                link_mask(V.tensor_scalar(above, wk[:, :], lo_c[R, :], steps[R, ROUNDS - 1:ROUNDS],
                                          ALU.subtract, ALU.is_ge), n, 1)
                link_mask(V.tensor_tensor(ties, at_least, above, ALU.subtract), n, 2)
                V.tensor_reduce(rowg_c[R, :], above, AX.X, ALU.add)
                V.tensor_reduce(rowe_c[R, :], ties, AX.X, ALU.add).then_inc(ties_ready, 1)

            def copy_ties(n):
                dve.wait_ge(ties_t, n + 1)
                V.tensor_copy(et[:, :], ps[0:MR_COLS, T_BANK, 0:MR_ROWS])
                V.tensor_copy(off_c[R, :], off_ps).then_inc(ties_copied, 1)

            def gates(n):
                dve.wait_ge(ties_scanned, n + 1)
                dve.wait_ge(ties_copied, n + 1)
                link_mask(V.tensor_scalar(keep, ps[R, T_BANK, C:C + MR_COLS], off_c[R, :], float(TOP),
                                          ALU.add, ALU.is_le), n, 3)
                link_mask(V.tensor_tensor(keep, keep, ties, ALU.mult), n, 4)
                link_mask(V.tensor_tensor(chosen, above, keep, ALU.add), n, 5)
                link_mask(V.tensor_tensor(gate, chosen, wk[:, :], ALU.mult), n, 6)
                link_mask(V.tensor_copy(mks[:, 0, :], gate), n, 7)
                V.tensor_tensor(mks[:, 1, :], gate, mks[:, 0, :].bitcast(f32), ALU.subtract).then_inc(gate_ready, 1)

            def apply_gate(m, b, c):
                g = m * NCH + c
                dve.wait_ge(bc_gate, g + 1)
                dve.wait_ge(y_taken, g + 1)
                V.tensor_tensor(cut(yo[b], c), cut(yo[b], c), ps[:, BC1, 0:T], ALU.mult).then_inc(gated, 1)

            def add_base(m, b, c):
                g = m * NCH + c
                dve.wait_ge(gated, g + 1)
                dve.wait_ge(base_ready, g + 1)
                V.tensor_tensor(cut(yo[b], c), cut(yo[b], c), cut(base[b], c), ALU.add).then_inc(out_ready, 1)

            def phase2(n, b):
                for pos in range(POS):
                    at = (n, b, pos)
                    rounds = due(COUNT_AT, 0, *at)
                    for m, mb, r in rounds:
                        choose(m, r)
                    for m, mb, _ in due(COUNT_AT[0] - 1, 0, *at):
                        count_above(m, 0)
                    for m, mb, _ in due(MASK_AT, 0, *at):
                        copy_ties(m)
                    for m, mb, _ in due(SCAN_AT, 0, *at):
                        gates(m)
                    low_hidden(dve, V, n, b, pos, False)
                    for m, mb, c in due(TRANSPOSE_AT, 1, *at):
                        tile_stats(m, c)
                    for m, mb, c in due(NORM_AT, 1, *at):
                        scale_tokens(m, mb, c)
                    for m, mb, r in rounds:
                        raise_end(m, r)
                    for m, mb, c in due([p + 1 for p in NORM_AT], 1, *at):
                        centre_tokens(m, mb, c)
                    for m, mb, _ in due(STAT_AT - 1, 1, *at):
                        mean_over_std(m)
                    for m, mb, c in due(OUT_AT, -1, *at):
                        apply_gate(m, mb, c)
                    for m, mb, r in rounds:
                        next_candidate(m, r)
                    for m, mb, _ in due(ROUTER_AT[-1] + 1, 0, *at):
                        take_router(m)
                    for m, mb, _ in due(VAR_AT, 1, *at):
                        token_variance(m)
                    for m, mb, _ in due(STAT_AT, 1, *at):
                        split_stats(m)
                    for m, mb, c in due([p + 1 for p in OUT_AT], -1, *at):
                        add_base(m, mb, c)
                    for m, mb, c in due(BASE_AT, 1, *at):
                        token_base(m, mb, c)
                    for m, mb, r in rounds:
                        if r + 1 < ROUNDS:
                            count_above(m, r + 1)
                        else:
                            find_ties(m)

            pairs(dve, phase2, *P2, -1, n_img + 1)

        @block.tensor
        def _(pe):
            M = nc.tensor.matmul
            pe.wait_ge(tables_ready, 2)
            pe.wait_ge(cw_signed, 1)
            for t in range(TAPS):
                wait_count(pe, cw_ready, t - 1)
                nc.tensor.transpose(ps[:, t % 2, 0:C // 2].bitcast(bf16), cws[:, t, :],
                                    ident_b[:, :]).then_inc(cw_transposed, 1)
            pe.wait_ge(cw_ready, TAPS)

            def centre(n, b, c):
                g = n * NCH + c
                pe.wait_ge(split_ready, g + 1)
                wait_count(pe, signed, g - 1)
                bank = ps[:, CEN_BANK + (b + c) % 2, 0:T]
                M(bank, centre_r[:, :], xh[(b + c) % 2][:, :], start=True, stop=False)
                M(bank, centre_r[:, :], xl[(b + c) % 2][:, :], start=False, stop=True).then_inc(centred, 1)

            def conv(n, b, c):
                g = n * NCH + c
                pe.wait_ge(signed, n * NCH + min(c + 2, NCH))
                wait_count(pe, y_copied, g - 1)
                bank = ps[:, CONV_BANK + (b + c) % 2, 0:T].rearrange("p (r w) -> p r w", w=SIDE)
                for t in range(TAPS):
                    dy, dx = divmod(t, 3)
                    last = M(bank, cwT[:, t, :], sg[b][:, c * ROWS + dy:c * ROWS + dy + ROWS, dx:dx + SIDE],
                             start=t == 0, stop=t == TAPS - 1)
                last.then_inc(conv_done, 1)

            for c in range(NCH):
                centre(0, 0, c)

            def phase1(n, b):
                for c in range(NCH):
                    conv(n, b, c)
                    if has(n + 1):
                        centre(n + 1, 1 - b, c)

            pairs(pe, phase1, *P1, 0, n_img)
            pe.wait_ge(wr2_ready, 1)
            M(ps[:, BC0, 0:1], kt[:, K_ONES:K_ONES + C], wr2, start=True, stop=True).then_inc(wr2_summed, 1)
            pe.wait_ge(y_copied, n_img * NCH)
            pe.wait_ge(bn_taken, n_img * NCH)

            def transposes(m, b, c, n, pos):
                pe.wait_ge(x1_ready, m * NCH + c + 1)
                wait_count(pe, t_ready if c % 2 else u_ready, done(NORM_AT, 1, n, pos))
                if c % 2:
                    wait_count(pe, gated, done(OUT_AT, -1, n, pos))
                if c > 1:
                    pe.wait_ge(stats_taken, m * NCH + c - 1)
                for i in range(TPG):
                    lo = c * T + i * TILE
                    last = nc.tensor.transpose(ps[0:TILE, BC0 + c % 2, i * C:(i + 1) * C], xb[b][:, lo:lo + TILE], ident)
                last.then_inc(transposed, 1)

            def router(n, b, c):
                pe.wait_ge(tl_ready, n * NCH + c + 1)
                if c == 0 and has(n - 1):
                    pe.wait_ge(mask_step, (n - 1) * MASK_STEPS + 3)
                bank = ps[:, T_BANK, 0:T]
                for i, (w, t) in enumerate(((wsel_h, th), (wsel_h, tl), (wsel_l, th))):
                    last = M(bank, w[:, C - c:2 * C - c], cut(t, c), start=c == 0 and i == 0,
                             stop=c == NCH - 1 and i == 2)
                if c == NCH - 1:
                    last.then_inc(w_done, 1)

            def rows_of_stats(m, n, pos):
                pe.wait_ge(mr_ready, m + 1)
                wait_count(pe, u_ready, done(NORM_AT, 1, n, pos))
                for q in range(2):
                    last = nc.tensor.transpose(ps[0:NT, BC0, q * C:q * C + TILE], rm[:, q, :],
                                               ident[0:TILE, 0:TILE])
                last.then_inc(stat_rows, 1)

            def spread_stats(m, b, c, n, pos):
                g = m * NCH + c
                if c == 0:
                    pe.wait_ge(norm_rows_in, (m + 1) * 64)
                wait_count(pe, u_ready, g)
                wait_count(pe, stats_taken, done(TRANSPOSE_AT, 1, n, pos + 1))
                wait_count(pe, rms_ready, done(STAT_AT, 1, n, pos + 1))
                M(ps[:, BC0, 0:T], ones_r[0:2, :], cut(rows[0:2, :], c), start=True, stop=True).then_inc(bc_stats, 1)
                wait_count(pe, t_ready, g)
                wait_count(pe, gated, done(OUT_AT, -1, n, pos + 1))
                M(ps[:, BC1, 0:T], ones_r[32:34, :], cut(rows[32:34, :], c), start=True, stop=True).then_inc(bc_stats, 1)

            def spread_gates(m, b, c, n, pos):
                g = m * NCH + c
                if c == 0:
                    pe.wait_ge(gate_rows_in, (m + 1) * 32)
                wait_count(pe, gated, g)
                wait_count(pe, t_ready, done(NORM_AT, 1, n, pos))
                wait_count(pe, stats_taken, done(TRANSPOSE_AT, 1, n, pos + 1))
                M(ps[:, BC1, 0:T], ones_r[64:66, :], cut(rows[64:66, :], c), start=True, stop=True).then_inc(bc_gate, 1)

            def hidden(n, b, c, j):
                g = n * NCH + c
                if j == 0:
                    pe.wait_ge(tl_ready, g + 1)
                wait_count(pe, hh_ready, (g - 1) * NB + j + 1)
                bank = ps[:, H_BANK + j, 0:T]
                blk = slice(j * C, (j + 1) * C)
                M(bank, w1_h[:, blk], cut(th, c), start=True, stop=False)
                M(bank, w1_h[:, blk], cut(tl, c), start=False, stop=False)
                M(bank, w1_l[:, blk], cut(th, c), start=False, stop=True).then_inc(h_done, 1)

            def output(n, b, c, j):
                g = n * NCH + c
                if j == 0:
                    wait_count(pe, y_taken, g)
                first, final = j == 0, j == NB - 1
                bank = ps[:, Y_BANK, 0:T]
                wait_low(pe, n, c, j)
                high, low = hh[(b + c) % 2][:, j, :], hl[(b + c) % 2][:, j, :]
                M(bank, w2_h[:, j, :], high, start=first, stop=False)
                M(bank, w2_h[:, j, :], low, start=False, stop=False)
                last = M(bank, w2_l[:, j, :], high, start=False, stop=final)
                if j == NB - 1:
                    last.then_inc(y_done, 1)

            def sum_counts(n, r):
                pe.wait_ge(part_counts, n * ROUNDS + r + 1)
                if r == 0:
                    pe.wait_ge(w_taken, n + 1)
                M(cnt_ps, cnt_c[:, :].to_broadcast([C, C]), cand_sel[:, :], start=True,
                  stop=True).then_inc(counts_summed, 1)

            def transpose_ties(n):
                pe.wait_ge(ties_ready, n + 1)
                R = slice(0, MR_ROWS)
                nc.tensor.transpose(ps[0:MR_COLS, T_BANK, 0:MR_ROWS], ties_sb, ident[R, R])
                M(off_ps, kt[R, K_ONES:K_ONES + MR_ROWS], rowg_c[R, :], start=True, stop=False)
                M(off_ps, kt[R, K_STRI:K_STRI + MR_ROWS], rowe_c[R, :], start=False, stop=True).then_inc(ties_t, 1)

            def scan_ties(n):
                pe.wait_ge(ties_copied, n + 1)
                M(ps[0:MR_ROWS, T_BANK, C:C + MR_COLS], et[:, :], kt[0:MR_COLS, K_TRIU:K_TRIU + MR_COLS],
                  start=True, stop=True).then_inc(ties_scanned, 1)

            def phase2(n, b):
                for pos in range(POS):
                    c, j = divmod(pos, 2 * NB)
                    if j < NB and has(n):
                        hidden(n, b, c, j)
                    if j >= NB and c > 0 and has(n):
                        output(n, b, c - 1, j - NB)
                    if j >= NB and c == 0 and has(n - 1):
                        output(n - 1, 1 - b, NCH - 1, j - NB)
                    at = (n, b, pos)
                    for m, mb, c in due(TRANSPOSE_AT, 1, *at):
                        transposes(m, mb, c, n, pos)
                    for m, mb, c in due(ROUTER_AT, 0, *at):
                        router(m, mb, c)
                    for m, mb, r in due(COUNT_AT, 0, *at):
                        sum_counts(m, r)
                    for m, mb, _ in due(MASK_AT, 0, *at):
                        transpose_ties(m)
                    for m, mb, _ in due(SCAN_AT, 0, *at):
                        scan_ties(m)
                    for m, mb, _ in due(STAT_AT, 1, *at):
                        rows_of_stats(m, n, pos)
                    for m, mb, c in due(OUT_AT, -1, *at):
                        spread_gates(m, mb, c, n, pos)
                    for m, mb, c in due(NORM_AT, 1, *at):
                        spread_stats(m, mb, c, n, pos)

            pairs(pe, phase2, *P2, -1, n_img + 1)


N_PARAMS = 12
_INS = ["x", "L0_conv_w", "L0_conv_b", "L0_conv_gamma", "L0_conv_beta", "L0_ffn_wr", "L0_ffn_br",
        "L0_ffn_w1", "L0_ffn_b1", "L0_ffn_w2", "L0_ffn_b2"]


def kernel(**inputs):
    import concourse.bacc as _bacc
    from concourse.bass_utils import run_bass_kernel_spmd as _run

    nc = _bacc.Bacc("TRN2", target_bir_lowering=False, num_devices=1)
    arrays = {"consts": constants()}
    for name in _INS:
        arrays[name] = np.ascontiguousarray(inputs[name])
    args = [nc.dram_tensor(name, a.shape, mybir.dt.from_np(a.dtype), kind="ExternalInput").ap()
            for name, a in arrays.items()]
    shape = arrays["x"].shape
    args.append(nc.dram_tensor("result", shape, mybir.dt.float32, kind="ExternalOutput").ap())
    block_kernel(nc, *args, shape[0])
    r = _run(nc, [arrays], core_ids=[0])
    return r.results[0]["result"]
```
